# Optimizing a Trainium2 kernel written in Bass

```python
import numpy as np
import jax
import jax.numpy as jnp

def _softmax(x, axis=-1):
    return jax.nn.softmax(x, axis=axis)

def _gelu(x):
    return jax.nn.gelu(x, approximate=True)

def _silu(x):
    return jax.nn.silu(x)

def _sigmoid(x):
    return jax.nn.sigmoid(x)

def _layernorm(x, axis=-1, eps=1e-05):
    m = jnp.mean(x, axis=axis, keepdims=True)
    v = jnp.var(x, axis=axis, keepdims=True)
    return (x - m) / jnp.sqrt(v + eps)

def _scatter_add(tgt, idx, src, axis=0):
    return tgt.at[idx].add(src)

def _segment_sum(src, seg, n):
    return jax.ops.segment_sum(src, seg, n)
kernel_name = 'mk_rec_standalone_d1_rec_r8_a6d737'

def setup_inputs(seed: int=0):
    np.random.seed(seed)
    _w = jnp.asarray

    def _rec_inputs():
        import jax
        import jax.numpy as jnp
        _rk = jax.random.key(seed)
        r_x = -0.000112629 + 1.00026 * jax.random.normal(jax.random.fold_in(_rk, 1), (1024, 50, 300), jnp.float32)
        r_label_embedding = -1.64977e-06 + 0.999867 * jax.random.normal(jax.random.fold_in(_rk, 2), (1024, 200, 300), jnp.float32)
        return (r_x, r_label_embedding)
    r_x, r_label_embedding = _rec_inputs()

    def _L0_rec_setup():
        import jax, jax.numpy as jnp
        import numpy as np
        E, U, C, T, N, B, K = (300, 300, 4, 8, 50, 512, 200)
        P = E * (E - 1) // 2
        PAD = jnp.float32(-2 ** 32 + 1)

        def _attn_pool(x, mask, w_a, b_a, w_b):
            score = jnp.exp((x @ w_a + b_a) @ w_b)
            score = jnp.where(mask == 0, PAD, score)
            p = jax.nn.softmax(score, axis=1)
            return jnp.einsum('bne,bn->be', x, p[..., 0])
        key = jax.random.key(seed)
        ks = jax.random.split(key, 20)
        s = 0.02
        return {'x': jax.random.normal(ks[0], (B, N, E), jnp.float32), 'label_embedding': jax.random.normal(ks[1], (B, K, U), jnp.float32), 'w1': jax.random.normal(ks[2], (E, T), jnp.float32) * s, 'b1': jnp.zeros((T,), jnp.float32), 'w2': jax.random.normal(ks[3], (T, 1), jnp.float32) * s, 'w3': jax.random.normal(ks[4], (E, T), jnp.float32) * s, 'b3': jnp.zeros((T,), jnp.float32), 'w4': jax.random.normal(ks[5], (T, 1), jnp.float32) * s, 'w5': jax.random.normal(ks[6], (2 * E, E), jnp.float32) * s, 'b5': jnp.zeros((E,), jnp.float32), 'w6': jax.random.normal(ks[7], (E, E), jnp.float32) * s, 'b6': jnp.zeros((E,), jnp.float32), 'w7': jax.random.normal(ks[8], (P, E), jnp.float32) * s, 'b7': jnp.zeros((E,), jnp.float32), 'w8': jax.random.normal(ks[9], (2 * E, U), jnp.float32) * s, 'b8': jnp.zeros((U,), jnp.float32), 'v': jax.random.uniform(ks[10], (E, C), jnp.float32)}
    _L0_rec_all = _L0_rec_setup()
    _L0_rec_in = {k: v for k, v in _L0_rec_all.items() if k in ('w1', 'b1', 'w2', 'w3', 'b3', 'w4', 'w5', 'b5', 'w6', 'b6', 'w7', 'b7', 'w8', 'b8', 'v')}
    del _L0_rec_all
    return {'r_x': r_x, 'r_label_embedding': r_label_embedding, 'L0_rec_w1': _L0_rec_in['w1'], 'L0_rec_b1': _L0_rec_in['b1'], 'L0_rec_w2': _L0_rec_in['w2'], 'L0_rec_w3': _L0_rec_in['w3'], 'L0_rec_b3': _L0_rec_in['b3'], 'L0_rec_w4': _L0_rec_in['w4'], 'L0_rec_w5': _L0_rec_in['w5'], 'L0_rec_b5': _L0_rec_in['b5'], 'L0_rec_w6': _L0_rec_in['w6'], 'L0_rec_b6': _L0_rec_in['b6'], 'L0_rec_w7': _L0_rec_in['w7'], 'L0_rec_b7': _L0_rec_in['b7'], 'L0_rec_w8': _L0_rec_in['w8'], 'L0_rec_b8': _L0_rec_in['b8'], 'L0_rec_v': _L0_rec_in['v']}

def reference(r_x, r_label_embedding, L0_rec_w1, L0_rec_b1, L0_rec_w2, L0_rec_w3, L0_rec_b3, L0_rec_w4, L0_rec_w5, L0_rec_b5, L0_rec_w6, L0_rec_b6, L0_rec_w7, L0_rec_b7, L0_rec_w8, L0_rec_b8, L0_rec_v):
    import jax
    import jax.numpy as jnp

    def _L0_rec_ref(x, label_embedding, w1, b1, w2, w3, b3, w4, w5, b5, w6, b6, w7, b7, w8, b8, v):
        import jax, jax.numpy as jnp
        import numpy as np
        E, U, C, T, N, B, K = (300, 300, 4, 8, 50, 512, 200)
        P = E * (E - 1) // 2
        PAD = jnp.float32(-2 ** 32 + 1)

        def _attn_pool(x, mask, w_a, b_a, w_b):
            score = jnp.exp((x @ w_a + b_a) @ w_b)
            score = jnp.where(mask == 0, PAD, score)
            p = jax.nn.softmax(score, axis=1)
            return jnp.einsum('bne,bn->be', x, p[..., 0])
        mask = jnp.sign(jnp.sum(jnp.abs(x), axis=2))[..., None]
        q1 = _attn_pool(x, mask, w1, b1, w2)
        q2 = _attn_pool(x, mask, w3, b3, w4)
        h = jnp.concatenate([q1, q2], axis=1) @ w5 + b5
        f6 = h @ w6 + b6
        iu, ju = jnp.triu_indices(E, k=1)
        g = (v @ v.T)[iu, ju]
        cross = h[:, iu] * h[:, ju] * g
        f7 = cross @ w7 + b7
        out8 = jnp.concatenate([f6, f7], axis=1) @ w8 + b8
        return jnp.einsum('bu,bku->bk', out8, label_embedding)
    y = _L0_rec_ref(r_x, r_label_embedding, L0_rec_w1, L0_rec_b1, L0_rec_w2, L0_rec_w3, L0_rec_b3, L0_rec_w4, L0_rec_w5, L0_rec_b5, L0_rec_w6, L0_rec_b6, L0_rec_w7, L0_rec_b7, L0_rec_w8, L0_rec_b8, L0_rec_v)
    return y

_drawn_inputs = setup_inputs


def setup_inputs(seed=0):
    import zlib

    import numpy as np

    out = dict(_drawn_inputs(seed))
    spreads = {'L0_rec_b1': (0.0, 0.8),
     'L0_rec_b3': (0.0, 0.8),
     'L0_rec_b5': (0.0, 0.1),
     'L0_rec_b6': (0.0, 0.1),
     'L0_rec_b7': (0.0, 0.1),
     'L0_rec_b8': (0.0, 0.1)}
    factors = {'L0_rec_w1': 8.0, 'L0_rec_w2': 8.0, 'L0_rec_w3': 8.0, 'L0_rec_w4': 8.0}
    for name, (base, spread) in spreads.items():
        noise = np.random.default_rng([zlib.crc32(name.encode()), seed]).standard_normal(out[name].shape)
        drawn = base * np.exp(spread * noise) if base else spread * noise
        out[name] = jnp.asarray(drawn.astype(out[name].dtype))
    for name, factor in factors.items():
        out[name] = (out[name] * factor).astype(out[name].dtype)
    return out
```

```python
from contextlib import ExitStack

import concourse.bass as bass
from concourse import mybir

F32 = mybir.dt.float32
U32 = mybir.dt.uint32
BF16 = mybir.dt.bfloat16
ALU = mybir.AluOpType
ACT = mybir.ActivationFunctionType
AX = mybir.AxisListType

P = 128
PAD = float(-2 ** 32 + 1)


def rec_kernel(nc, x, label, w1, b1, w2, w3, b3, w4, w5, b5, w6, b6, w7, b7, w8, b8, v, out):
    B, N, E = x.shape
    K = label.shape[1]
    HID = w1.shape[1]
    VC = v.shape[1]
    PAIRS = E * (E - 1) // 2
    NBT = B // P
    CHUNKS = [(c * P, min(P, E - c * P)) for c in range((E + P - 1) // P)]
    NCH = len(CHUNKS)

    UB = P // 2
    T = N // 2
    NS = B // UB
    XSLOTS = 4
    DG, AG = 4, 2
    DGS, AGS = -(-T // DG), -(-T // AG)
    assert DGS % 2 == 1 and AGS % 2 == 1
    KB = 13
    BLK = P * KB
    NBLK = (PAIRS + BLK - 1) // BLK
    LASTP = (PAIRS - (NBLK - 1) * BLK) // KB
    assert LASTP * KB == PAIRS - (NBLK - 1) * BLK and NBLK % 2 == 1
    GROUPS = [(0, 3), (3, 3), (6, 2)]
    NB = max(n for _, n in GROUPS)
    LR = 10
    LC = K // LR
    LSLOTS = 5
    assert LC % LSLOTS == 0

    row_start = [i * (E - 1) - i * (i - 1) // 2 for i in range(E)]

    ctx = ExitStack()
    with ctx:
        def sb(name, shape, dt=F32):
            return ctx.enter_context(nc.sbuf_tensor(name, shape, dt))

        def sem(name):
            return ctx.enter_context(nc.semaphore(name))

        stream = sb("stream", [P, 3 * T * E])
        w7ring = sb("w7ring", [P, 2 * KB * E])
        cross = sb("cross", [P, 2 * NB * BLK])
        xslot = [stream[:, k * T * E:(k + 1) * T * E] for k in range(3)] + [w7ring[:, 0:T * E]]
        xslot = [a.rearrange("p (t e) -> p t e", e=E) for a in xslot]
        lslot = [stream[:, k * LR * E:(k + 1) * LR * E].rearrange("p (r e) -> p r e", e=E)
                 for k in range(LSLOTS)]
        w7blk = [w7ring[:, k * KB * E:(k + 1) * KB * E] for k in range(2)]
        cblk = [cross[:, k * NB * BLK:(k + 1) * NB * BLK].rearrange("p (b c) -> p b c", c=BLK)
                for k in range(2)]
        at = [0]

        def take(cols):
            at[0] += cols
            assert at[0] <= 2 * NB * BLK
            return cross[:, at[0] - cols:at[0]]

        weights = [take(T * P).rearrange("p (t h b) -> p t h b", t=T, h=2) for _ in range(2)]
        w5sb = take(2 * NCH * E).rearrange("p (c e) -> p c e", e=E)
        w6sb = take(NCH * E).rearrange("p (c e) -> p c e", e=E)
        ubc = take(2 * (E + 1)).rearrange("p (h e) -> p h e", h=2)
        onehot = take(UB)

        gram = sb("gram", [P, NCH, E])
        w8sb = sb("w8sb", [P, 2 * NCH, E])
        h_all = sb("h_all", [P, NBT, E])
        out8 = sb("out8", [P, NBT, E])
        rest = stream[:, LSLOTS * LR * E:3 * T * E]
        score = rest[:, 0:NBT * K].rearrange("p (m k) -> p m k", k=K)
        gcol = sb("gcol", [P, NBLK, KB])
        cT = [rest[:, NBT * K + k * NB * P:NBT * K + (k + 1) * NB * P] for k in range(2)]
        ident = sb("ident", [P, P])
        ones = sb("ones", [P, P])
        brow = sb("brow", [P, E])
        products = sb("products", [P, 2, DG, E], BF16)
        padv = sb("padv", [P, 1])
        tick = sb("tick", [P, 1])
        turnT = sb("turnT", [P, NCH, 2, P])
        turn1 = turnT[:].rearrange("p c h b -> p (c h b)")[:, 0:NCH * P].rearrange("p (c b) -> p c b", c=NCH)
        flat = sb("flat", [P, max(NB, 4), E])
        small = sb("small", [P, XSLOTS, 2, 3 * T + 8])
        w1nat = sb("w1nat", [P, 2, NCH, HID])
        vnat = sb("vnat", [P, NCH, VC])
        w1T = flat[0:HID, 0:3, :].rearrange("p a e -> p (a e)")[:, 0:2 * (E + 1)].rearrange(
            "p (h e) -> p h e", h=2)
        vT = products[0:VC].rearrange("p a b e -> p (a b e)")[:, 0:2 * E].bitcast(F32)
        w2sb = sb("w2sb", [HID, 2])
        w2bc = sb("w2bc", [HID, 2, P])
        gflat = nc.dram_tensor("g_flat", [1, PAIRS], F32, kind="Internal").ap()

        dots = [small[:, k, :, 0:T] for k in range(XSLOTS)]
        expo = [small[:, k, :, T:2 * T] for k in range(XSLOTS)]
        prob = [small[:, k, :, 2 * T:3 * T] for k in range(XSLOTS)]
        maxi = [small[:, k, :, 3 * T:3 * T + 1] for k in range(XSLOTS)]
        maxo = [small[:, k, :, 3 * T + 1:3 * T + 2] for k in range(XSLOTS)]
        nmax = [small[:, k, :, 3 * T + 2:3 * T + 3] for k in range(XSLOTS)]
        part = [small[:, k, :, 3 * T + 3:3 * T + 4] for k in range(XSLOTS)]
        parto = [small[:, k, :, 3 * T + 4:3 * T + 5] for k in range(XSLOTS)]
        total = [small[:, k, :, 3 * T + 5:3 * T + 6] for k in range(XSLOTS)]
        recip = [small[:, k, :, 3 * T + 6:3 * T + 7] for k in range(XSLOTS)]
        absum = sb("absum", [P, XSLOTS, T])
        masked = sb("masked", [P, XSLOTS, T])

        bank = [ctx.enter_context(nc.psum_tensor(f"bank{k}", [P, 512], F32)) for k in range(8)]
        acc = bank[0:NB]
        turned = bank[4:6]
        side = bank[6:8]
        absolutes = bank[2:6]

        small_in = sem("small_in")
        w_in = sem("w_in")
        consts = sem("consts")
        vconsts = sem("vconsts")
        set_mm = sem("set_mm")
        set_ev = sem("set_ev")
        g_stored = sem("g_stored")
        g_in = sem("g_in")
        x_in = [sem(f"x_in{k}") for k in range(XSLOTS)]
        x_free = sem("x_free")
        dots_done = sem("dots_done")
        abs_done = sem("abs_done")
        exp_done = sem("exp_done")
        max_done = sem("max_done")
        prob_raw = sem("prob_raw")
        prob_done = sem("prob_done")
        weights_done = sem("weights_done")
        pool_out = sem("pool_out")
        chain_mm = sem("chain_mm")
        chain_ev = sem("chain_ev")
        link = sem("link")
        c_ready = sem("c_ready")
        c_used = sem("c_used")
        w7_in = [sem(f"w7_in{k}") for k in range(2)]
        w7_used = sem("w7_used")
        turned_done = sem("turned_done")
        cT_done = sem("cT_done")
        acc_done = sem("acc_done")
        f7_out = sem("f7_out")
        end_mm = sem("end_mm")
        end_ev = sem("end_ev")
        l_in = [sem(f"l_in{k}") for k in range(LSLOTS)]
        l_used = sem("l_used")
        out_stored = sem("out_stored")

        STEPS = (1, 6)
        CH_BT = sum(STEPS)
        SMALL_LOADS = 3 * 2 + 2 + 2
        W_LOADS = 5 * 2 + 4

        def at_tile(t, m):
            return t[:, m, :] if isinstance(m, int) else t[:, bass.ds(m, 1), :].rearrange("p o e -> p (o e)")

        x_v = x.rearrange("(s b) (f t) e -> s (b f) (t e)", b=UB, f=2)
        label_v = label.rearrange("(m p) (c r) e -> m p c (r e)", p=P, r=LR)
        out_v = out.rearrange("(m p) k -> m p k", p=P)
        row = lambda a: a.rearrange("(o e) -> o e", o=1)
        col = lambda a: a.rearrange("(e o) -> e o", o=1)

        block = ctx.enter_context(nc.Block())

        @block.sync
        def _(sp):
            def rows_in(dst, src, s):
                full = E // P
                sp.dma_start(dst[:, 0:full, :], src[0:full * P, :].rearrange("(c p) n -> p c n", p=P)).then_inc(s, 16)
                sp.dma_start(dst[0:E - full * P, full, :], src[full * P:E, :]).then_inc(s, 16)

            rows_in(w1nat[:, 0], w1, small_in)
            rows_in(w1nat[:, 1], w3, small_in)
            rows_in(vnat[:], v, small_in)
            sp.dma_start(w2sb[:, 0:1], w2).then_inc(small_in, 16)
            sp.dma_start(w2sb[:, 1:2], w4).then_inc(small_in, 16)
            sp.dma_start(w1T[:, 0, E:E + 1], col(b1)).then_inc(small_in, 16)
            sp.dma_start(w1T[:, 1, E:E + 1], col(b3)).then_inc(small_in, 16)
            for n in range(XSLOTS):
                sp.dma_start(xslot[n], x_v[n]).then_inc(x_in[n], 16)
            rows_in(w5sb[:, 0:NCH], w5[0:E, :], w_in)
            rows_in(w5sb[:, NCH:2 * NCH], w5[E:2 * E, :], w_in)
            rows_in(w6sb, w6, w_in)
            rows_in(w8sb[:, 0:NCH], w8[0:E, :], w_in)
            rows_in(w8sb[:, NCH:2 * NCH], w8[E:2 * E, :], w_in)
            for k, b in enumerate((b5, b6, b8, b7)):
                sp.dma_start(brow[32 * k:32 * k + 1, :], row(b)).then_inc(w_in, 16)

            sp.wait_ge(set_ev, 5 + NCH)
            for i in range(E - 1):
                sp.dma_start(gflat[:, row_start[i]:row_start[i + 1]],
                             gram[i % P:i % P + 1, i // P, i + 1:E]).then_inc(g_stored, 16)

            with sp.Fori(1, NS // XSLOTS) as i:
                for k in range(XSLOTS):
                    sp.wait_ge(x_free, (i - 1) * XSLOTS + k + 1)
                    sp.dma_start(xslot[k], x_v[bass.ds(i * XSLOTS + k, 1)].rearrange("o p c -> (o p) c")
                                 ).then_inc(x_in[k], 16)

            sp.wait_ge(g_stored, 16 * (E - 1))
            sp.wait_ge(consts, 1)
            full = (NBLK - 1) * BLK
            sp.dma_start(gcol[:, 0:NBLK - 1, :],
                         gflat[:, 0:full].rearrange("o (n p k) -> p (o n) k", p=P, k=KB)).then_inc(g_in, 16)
            sp.dma_start(gcol[0:LASTP, NBLK - 1, :],
                         gflat[:, full:PAIRS].rearrange("o (p k) -> (o p) k", k=KB)).then_inc(g_in, 16)

            sp.wait_ge(x_free, NS)
            for c in range(LSLOTS):
                sp.dma_start(lslot[c], label_v[0, :, c]).then_inc(l_in[c], 16)
            for c in range(LSLOTS, LC):
                sp.wait_ge(l_used, c - LSLOTS + 1)
                sp.dma_start(lslot[c % LSLOTS], label_v[0, :, c]).then_inc(l_in[c % LSLOTS], 16)
            with sp.Fori(1, NBT) as m:
                for c in range(LC):
                    sp.wait_ge(l_used, m * LC + (c - LSLOTS + 1))
                    sp.dma_start(lslot[c % LSLOTS], label_v[bass.ds(m, 1), :, c].rearrange("o p c -> (o p) c")
                                 ).then_inc(l_in[c % LSLOTS], 16)

        @block.gpsimd
        def _(pool):
            ki = [0]

            def step(ins):
                ki[0] += 1
                ins.then_inc(consts, 1)
                pool.wait_ge(consts, ki[0])

            step(nc.gpsimd.memset(gcol[:], 0.0))
            step(nc.gpsimd.memset(ident[:], 0.0))
            step(nc.gpsimd.memset(onehot, 0.0))
            step(nc.gpsimd.affine_select(out=ident[:], in_=ident[:], compare_op=ALU.not_equal, fill=1.0,
                                         base=0, pattern=[[-1, P]], channel_multiplier=1))
            for f in range(2):
                step(nc.gpsimd.affine_select(out=onehot, in_=onehot, compare_op=ALU.not_equal,
                                             fill=1.0, base=-f, pattern=[[-2, UB]], channel_multiplier=1))

            def spread(n, k, wait_free):
                pool.wait_ge(prob_done, n + 1)
                if wait_free:
                    pool.wait_ge(x_free, n - 1)
                nc.gpsimd.tensor_tensor(
                    weights[k % 2],
                    prob[k].rearrange("p h t -> p t h").unsqueeze(3).to_broadcast([P, T, 2, UB]),
                    onehot.unsqueeze(1).unsqueeze(1).to_broadcast([P, T, 2, UB]),
                    ALU.mult).then_inc(weights_done, 1)

            for n in range(XSLOTS):
                spread(n, n, n >= 2)
            with pool.Fori(1, NS // XSLOTS) as i:
                for k in range(XSLOTS):
                    spread(i * XSLOTS + k, k, True)

            with pool.Fori(0, NBT) as m:
                pool.wait_ge(l_used, m * LC + LC)
                pool.dma_start(out_v[bass.ds(m, 1)].rearrange("o p k -> (o p) k"),
                               score[:, bass.ds(m, 1), :].rearrange("p o k -> p (o k)")).then_inc(out_stored, 16)
            pool.wait_ge(out_stored, 16 * NBT)

        @block.tensor
        def _(pe):
            pe.wait_ge(consts, 6)
            pe.wait_ge(small_in, 16 * SMALL_LOADS)
            for hd in range(2):
                for c, (o, n) in enumerate(CHUNKS):
                    mm = pe.transpose(bank[2 + hd][0:HID, o:o + n], w1nat[0:n, hd, c, :], ident[0:n, 0:n])
                mm.then_inc(set_mm, 1)
            for c, (o, n) in enumerate(CHUNKS):
                mm = pe.transpose(bank[4][0:VC, o:o + n], vnat[0:n, c, :], ident[0:n, 0:n])
            mm.then_inc(set_mm, 1)
            pe.wait_ge(set_ev, 3)
            pe.wait_ge(vconsts, 3)
            for hd in range(2):
                pe.matmul(bank[6 + hd][:, 0:E + 1], w2bc[:, hd, :], w1T[:, hd, :],
                          start=True, stop=True).then_inc(set_mm, 1)
            for c, (o, n) in enumerate(CHUNKS):
                pe.matmul(bank[2 + c][0:n, 0:E], vT[:, o:o + n], vT, start=True, stop=True).then_inc(set_mm, 1)

            def tturn(dst, src):
                for c, (o, n) in enumerate(CHUNKS):
                    mm = pe.transpose(dst[0:n, c * P:(c + 1) * P], src[:, o:o + n], ident[:])
                return mm

            def spread_row(dst, k):
                o = 32 * k
                return pe.matmul(dst[:, 0:E], ones[o:o + 1, :], brow[o:o + 1, :], start=True, stop=False)

            def rows_mm(dst, lhs, rhs, bias, nlhs):
                mm = spread_row(dst, bias)
                for q in range(nlhs):
                    n = CHUNKS[q % NCH][1]
                    mm = pe.matmul(dst[:, 0:E], lhs(q)[0:n, :], rhs[0:n, q, :], start=False, stop=(q == nlhs - 1))
                return mm

            def chain(m, s, step):
                if step == 0:
                    pe.wait_ge(pool_out, m * 2 + s + 1)
                pe.wait_ge(chain_ev, m * CH_BT + s + step)
                dst = side[step % 2]
                if step == 0:
                    mm = tturn(dst, flat[:, s, :])
                elif step == 1:
                    mm = rows_mm(dst, lambda q: turnT[:, q % NCH, q // NCH, :], w5sb, 0, 2 * NCH)
                elif step == 2:
                    mm = tturn(dst, flat[:, 3, :])
                elif step == 3:
                    mm = rows_mm(dst, lambda q: turn1[:, q, :], w6sb, 1, NCH)
                elif step == 4:
                    mm = tturn(dst, flat[:, 2, :])
                else:
                    mm = rows_mm(dst, lambda q: turn1[:, q, :], w8sb, 2, NCH)
                mm.then_inc(chain_mm, 1)

            def pool_tile(n, k):
                pe.wait_ge(weights_done, n + 1)
                for t in range(T):
                    mm = pe.matmul(bank[k % 2][:, 0:E], weights[k % 2][:, t], xslot[k][:, t, :],
                                   start=(t == 0), stop=(t == T - 1))
                mm.then_inc(x_free, 1)

            def half_chain(m, s):
                for step in range(STEPS[s]):
                    chain(m, s, step)

            pe.wait_ge(w_in, 16 * W_LOADS)
            pe.wait_ge(set_ev, 5 + NCH)
            pool_tile(0, 0)
            for n in range(1, XSLOTS):
                half_chain((n - 1) // 2, (n - 1) % 2)
                pool_tile(n, n)
            with pe.Fori(1, NS // XSLOTS) as i:
                for k in range(XSLOTS):
                    half_chain(i * 2 + (k - 1) // 2, (k - 1) % 2)
                    pool_tile(i * XSLOTS + k, k)
            half_chain(NBT - 1, 1)

            loads = [0, 0]
            for g, (b0, nb) in enumerate(GROUPS):
                blk0, tile0 = g * NBLK, g * NBLK * KB

                def turn(blk, k):
                    if k == 0:
                        pe.wait_ge(c_ready, blk[0] + (blk0 + blk[1] + 1))
                    q = (tile0 + blk[1] * KB + k) % 2
                    for b in range(nb):
                        mm = pe.transpose(turned[q][:, b * P:(b + 1) * P],
                                          cblk[(blk0 + blk[1]) % 2][:, b, k:BLK:KB], ident[:])
                    mm.then_inc(turned_done, 1)

                def contract(blk, tiles, k, landed, np_):
                    slot, q = (blk0 + blk) % 2, (tile0 + blk * KB + k) % 2
                    last = landed is not None and np_ < P and k == KB - 1
                    if k == 0:
                        pe.wait_ge(w7_in[slot], landed)
                    pe.wait_ge(cT_done, tiles + (tile0 + blk * KB + k + 1))
                    for b in range(nb):
                        mm = pe.matmul(acc[b][:, 0:E], cT[q][0:np_, b * P:(b + 1) * P],
                                       w7blk[slot][0:np_, k * E:(k + 1) * E], start=False, stop=last)
                    if last:
                        mm.then_inc(acc_done, 1)
                    elif k == KB - 1:
                        mm.then_inc(w7_used, 1)
                    elif k == KB - 2:
                        mm.then_inc(c_used, 1)

                if g == 0:
                    pe.wait_ge(chain_ev, CH_BT * NBT)
                else:
                    pe.wait_ge(f7_out, b0)
                for b in range(nb):
                    mm = spread_row(acc[b], 3)
                if g == 0:
                    mm.then_inc(w7_used, 1)
                turn((0, 0), 0)
                s0, s1 = blk0 % 2, (blk0 + 1) % 2
                with pe.Fori(0, NBLK // 2) as i:
                    for par in range(2):
                        for k in range(KB):
                            turn((i * 2, par), k + 1) if k + 1 < KB else turn((i * 2, par + 1), 0)
                            contract(par, i * (2 * KB), k, (i + (loads[(s0, s1)[par]] + 1)) * 16, P)
                for k in range(KB):
                    if k + 1 < KB:
                        turn((0, NBLK - 1), k + 1)
                    contract(NBLK - 1, 0, k, 16 * (loads[s0] + NBLK // 2 + 2), LASTP)
                loads[s0] += NBLK // 2 + 2
                loads[s1] += NBLK // 2

                for b in range(nb):
                    e = 2 * (b0 + b)
                    pe.wait_ge(f7_out, b0 + b + 1)
                    if e:
                        pe.wait_ge(end_ev, e)
                    tturn(side[0], flat[:, b, :]).then_inc(end_mm, 1)
                    pe.wait_ge(end_ev, e + 1)
                    pe.matmul(side[1][:, 0:E], ident[:], out8[:, b0 + b, :], start=True, stop=False)
                    for c, (_, n) in enumerate(CHUNKS):
                        mm = pe.matmul(side[1][:, 0:E], turn1[0:n, c, :], w8sb[0:n, NCH + c, :],
                                       start=False, stop=(c == NCH - 1))
                    mm.then_inc(end_mm, 1)

        @block.scalar
        def _(act):
            def cp(dst, src):
                return nc.scalar.activation(dst, src, ACT.Copy)

            def absolute(n, k, t):
                grp, r = t // AG, t % AG
                if r == 0 and not (isinstance(n, int) and n * AGS + grp < 2):
                    act.wait_ge(abs_done, n * AGS + grp - 1)
                ins = nc.scalar.activation(absolutes[(k + grp) % 2 * AG + r][:, 0:E], xslot[k][:, t, :],
                                           ACT.Abs, accum_out=absum[:, k, t:t + 1])
                if r == AG - 1 or t == T - 1:
                    ins.then_inc(abs_done, 1)

            def exps(n, k):
                act.wait_ge(dots_done, (n + 1) * (2 * DGS))
                for hd in range(2):
                    ins = nc.scalar.activation(expo[k][:, hd, :], dots[k][:, hd, :], ACT.Exp,
                                               bias=ubc[:, hd, E:E + 1])
                ins.then_inc(exp_done, 1)

            def softexp(n, k):
                act.wait_ge(max_done, n + 1)
                for hd in range(2):
                    ins = nc.scalar.activation(prob[k][:, hd, :], expo[k][:, hd, :], ACT.Exp,
                                               bias=nmax[k][:, hd, :], accum_out=part[k][:, hd, :])
                ins.then_inc(prob_raw, 1)

            def turned_out(dst3, src):
                cp(dst3[:, 0:NCH - 1], src[:, 0:(NCH - 1) * P].rearrange("p (c b) -> p c b", b=P))
                n = CHUNKS[-1][1]
                return cp(dst3[0:n, NCH - 1], src[0:n, (NCH - 1) * P:NCH * P])

            def pools_turned(src, s):
                for c, (_, n) in enumerate(CHUNKS):
                    ins = cp(turnT[0:n, c, :, s * UB:(s + 1) * UB],
                             src[0:n, c * P:(c + 1) * P].rearrange("p (h b) -> p h b", h=2))
                return ins

            def chain_out(m, s, step):
                act.wait_ge(chain_mm, m * CH_BT + (s + step + 1))
                src = side[step % 2]
                if step == 0:
                    ins = pools_turned(src, s)
                elif step == 1:
                    cp(at_tile(h_all, m), src[:, 0:E])
                    ins = cp(flat[:, 3, :], src[:, 0:E])
                elif step == 3:
                    ins = cp(flat[:, 2, :], src[:, 0:E])
                elif step == 5:
                    ins = cp(at_tile(out8, m), src[:, 0:E])
                else:
                    ins = turned_out(turn1, src)
                ins.then_inc(chain_ev, 1)

            def pools_out(m, s):
                act.wait_ge(x_free, m * 2 + (s + 1))
                cp(flat[:, s, :], bank[s][:, 0:E]).then_inc(pool_out, 1)

            def tile(n, k, nxt_in, m):
                exps(n, k)
                chains = [] if m is None else list(range(STEPS[k % 2]))
                if m is not None:
                    pools_out(m, k % 2)
                if nxt_in is not None:
                    act.wait_ge(x_in[(k + 1) % XSLOTS], nxt_in)
                for t in range(T):
                    if nxt_in is not None:
                        absolute(n + 1, (k + 1) % XSLOTS, t)
                    if t % 2 == 1 and chains:
                        chain_out(m, k % 2, chains.pop(0))
                    if t == T // 2:
                        softexp(n, k)

            act.wait_ge(set_ev, 5 + NCH)
            act.wait_ge(x_in[0], 16)
            for t in range(T):
                absolute(0, 0, t)
            for n in range(XSLOTS):
                tile(n, n, 16 if n < XSLOTS - 1 else 32, None if n < 2 else 0)
            with act.Fori(1, NS // XSLOTS - 1) as i:
                for k in range(XSLOTS):
                    tile(i * XSLOTS + k, k, (i + 1) * 16 if k < XSLOTS - 1 else (i + 2) * 16,
                         i * 2 + (k // 2 - 1))
            for k in range(XSLOTS):
                tile(NS - XSLOTS + k, k, 16 * (NS // XSLOTS) if k < XSLOTS - 1 else None,
                     NBT - 2 + k // 2 - 1)
            for s in range(2):
                pools_out(NBT - 1, s)
                for step in range(STEPS[s]):
                    chain_out(NBT - 1, s, step)

            act.wait_ge(g_in, 32)
            full = (NBLK - 1) * BLK
            w7_v = w7[0:full, :].rearrange("(n p k) e -> n p (k e)", p=P, k=KB)
            w7_last = w7[full:PAIRS, :].rearrange("(p k) e -> p (k e)", k=KB)

            def load(slot, blk):
                act.dma_start(w7blk[slot], w7_v[blk] if isinstance(blk, int) else
                              w7_v[bass.ds(blk, 1)].rearrange("o p c -> (o p) c")).then_inc(w7_in[slot], 16)

            def load_last(slot):
                cut = LASTP // 16 * 16
                act.dma_start(w7blk[slot][0:cut], w7_last[0:cut]).then_inc(w7_in[slot], 16)
                act.dma_start(w7blk[slot][cut:LASTP], w7_last[cut:LASTP]).then_inc(w7_in[slot], 16)

            act.wait_ge(chain_mm, CH_BT * NBT)
            load(0, 0)
            for g, (b0, nb) in enumerate(GROUPS):
                blk0, tile0, used = g * NBLK, g * NBLK * KB, g * (NBLK - 1)
                s0, s1 = blk0 % 2, (blk0 + 1) % 2

                def scaled(tiles, blk, k, gblk, np_):
                    act.wait_ge(turned_done, tiles + (tile0 + blk * KB + k + 1))
                    q = (tile0 + blk * KB + k) % 2
                    nc.scalar.activation(cT[q][0:np_, 0:nb * P], turned[q][0:np_, 0:nb * P], ACT.Copy,
                                         scale=gblk[0:np_, k:k + 1]).then_inc(cT_done, 1)

                with act.Fori(0, NBLK // 2 - 1) as i:
                    for par in range(2):
                        for k in range(KB):
                            scaled(i * (2 * KB), par, k, at_tile(gcol, i * 2 + par), P)
                            if k == 2 and par == 0:
                                act.wait_ge(w7_used, i * 2 + (used + 1))
                                load(s1, i * 2 + 1)
                            if k == 2 and par == 1:
                                act.wait_ge(w7_used, i * 2 + (used + 2))
                                load(s0, i * 2 + 2)
                for blk in range(NBLK - 3, NBLK):
                    for k in range(KB):
                        scaled(0, blk, k, gcol[:, blk, :], P if blk < NBLK - 1 else LASTP)
                        if k == 2:
                            act.wait_ge(w7_used, used + blk + 1)
                            if blk + 1 < NBLK - 1:
                                load(s1, blk + 1)
                            elif blk + 1 == NBLK - 1:
                                load_last(s0)
                            elif g + 1 < len(GROUPS):
                                load(s1, 0)

                act.wait_ge(acc_done, g + 1)
                for b in range(nb):
                    cp(flat[:, b, :], acc[b][:, 0:E]).then_inc(f7_out, 1)
                for b in range(nb):
                    e = 2 * (b0 + b)
                    act.wait_ge(end_mm, e + 1)
                    turned_out(turn1, side[0]).then_inc(end_ev, 1)
                    act.wait_ge(end_mm, e + 2)
                    cp(out8[:, b0 + b, :], side[1][:, 0:E]).then_inc(end_ev, 1)

        @block.vector
        def _(dve):
            nc.vector.memset(ones[:], 1.0).then_inc(vconsts, 1)
            nc.vector.memset(padv[:], PAD).then_inc(vconsts, 1)
            dve.wait_ge(small_in, 16 * SMALL_LOADS)
            nc.vector.tensor_copy(w2bc[:], w2sb[:].unsqueeze(2).to_broadcast([HID, 2, P])).then_inc(vconsts, 1)
            for hd in range(2):
                dve.wait_ge(set_mm, hd + 1)
                nc.vector.tensor_copy(w1T[:, hd, 0:E], bank[2 + hd][0:HID, 0:E]).then_inc(set_ev, 1)
            dve.wait_ge(set_mm, 3)
            nc.vector.tensor_copy(vT, bank[4][0:VC, 0:E]).then_inc(set_ev, 1)
            for hd in range(2):
                dve.wait_ge(set_mm, 4 + hd)
                nc.vector.tensor_copy(ubc[:, hd, :], bank[6 + hd][:, 0:E + 1]).then_inc(set_ev, 1)
            for c, (o, n) in enumerate(CHUNKS):
                dve.wait_ge(set_mm, 6 + c)
                nc.vector.tensor_copy(gram[0:n, c, :], bank[2 + c][0:n, 0:E]).then_inc(set_ev, 1)
            dve.wait_ge(set_ev, 5 + NCH)

            SWAP = [q ^ 1 for q in range(32)]

            def score_rows(n, k, hd, landed):
                if hd == 0:
                    dve.wait_ge(x_in[k], landed)
                for t in range(T):
                    grp, r = hd * DGS + t // DG, t % DG
                    if r == 0 and not (isinstance(n, int) and n * 2 * DGS + grp < 2):
                        dve.wait_ge(dots_done, n * (2 * DGS) + (grp - 1))
                    ins = nc.vector.scalar_tensor_tensor(
                        out=products[:, grp % 2, r, :], in0=xslot[k][:, t, :], scalar=1.0, in1=ubc[:, hd, 0:E],
                        op0=ALU.mult, op1=ALU.mult, accum_out=dots[k][:, hd, t:t + 1])
                    if r == DG - 1 or t == T - 1:
                        ins.then_inc(dots_done, 1)

            LINKS = 8

            def linked(ins, n, j):
                ins.then_inc(link, 1)
                dve.wait_ge(link, n * LINKS + j)

            def carry():
                nc.vector.memset(tick[:], 0.0)

            def maxima(n, k):
                dve.wait_ge(exp_done, n + 1)
                dve.wait_ge(abs_done, (n + 1) * AGS)
                linked(nc.vector.tensor_scalar(masked[:, k, :], absum[:, k, :], 0.0, None, ALU.is_equal), n, 1)
                carry()
                for hd in range(2):
                    ins = nc.vector.copy_predicated(expo[k][:, hd, :], masked[:, k, :].bitcast(U32),
                                                    padv[:].to_broadcast([P, T]))
                linked(ins, n, 2)
                linked(nc.vector.tensor_reduce(maxi[k], expo[k], AX.X, ALU.max), n, 3)
                carry()
                linked(nc.vector.stream_shuffle(maxo[k], maxi[k], SWAP), n, 4)
                linked(nc.vector.tensor_tensor(maxi[k], maxi[k], maxo[k], ALU.max), n, 5)
                nc.vector.tensor_scalar(nmax[k], maxi[k], -1.0, None, ALU.mult).then_inc(max_done, 1)

            def normalise(n, k):
                dve.wait_ge(prob_raw, n + 1)
                carry()
                linked(nc.vector.stream_shuffle(parto[k], part[k], SWAP), n, 6)
                linked(nc.vector.tensor_tensor(total[k], part[k], parto[k], ALU.add), n, 7)
                linked(nc.vector.reciprocal(recip[k], total[k]), n, 8)
                nc.vector.tensor_tensor(prob[k], prob[k], recip[k].to_broadcast([P, 2, T]),
                                        ALU.mult).then_inc(prob_done, 1)

            score_rows(0, 0, 0, 16)
            score_rows(0, 0, 1, 16)

            def tile(n, k, nxt_in):
                if nxt_in is not None:
                    score_rows(n + 1, (k + 1) % XSLOTS, 0, nxt_in)
                maxima(n, k)
                if nxt_in is not None:
                    score_rows(n + 1, (k + 1) % XSLOTS, 1, nxt_in)
                normalise(n, k)

            with dve.Fori(0, NS // XSLOTS - 1) as i:
                for k in range(XSLOTS):
                    tile(i * XSLOTS + k, k, (i + 1) * 16 if k < XSLOTS - 1 else (i + 2) * 16)
            for k in range(XSLOTS):
                tile(NS - XSLOTS + k, k, 16 * (NS // XSLOTS) if k < XSLOTS - 1 else None)

            def label_chunk(m, c):
                dve.wait_ge(l_in[c % LSLOTS], m * (16 * LC // LSLOTS) + 16 * (c // LSLOTS + 1))
                for r in range(LR):
                    ins = nc.vector.scalar_tensor_tensor(
                        out=lslot[c % LSLOTS][:, r, :], in0=lslot[c % LSLOTS][:, r, :], scalar=1.0, in1=at_tile(out8, m),
                        op0=ALU.mult, op1=ALU.mult, accum_out=at_tile(score, m)[:, c * LR + r:c * LR + r + 1])
                ins.then_inc(l_used, 1)

            def pair_block(b0, nb, slot, blk):
                lo = blk * BLK
                hi = min(lo + BLK, PAIRS)
                for i in range(E - 1):
                    a, z = max(lo, row_start[i]), min(hi, row_start[i + 1])
                    if a < z:
                        j = i + 1 + a - row_start[i]
                        ins = nc.vector.tensor_tensor(
                            cblk[slot][:, 0:nb, a - lo:z - lo], h_all[:, b0:b0 + nb, j:j + z - a],
                            h_all[:, b0:b0 + nb, i:i + 1].to_broadcast([P, nb, z - a]), ALU.mult)
                ins.then_inc(c_ready, 1)

            dve.wait_ge(chain_ev, CH_BT * NBT)
            dve.wait_ge(g_stored, 16 * (E - 1))
            for g, (b0, nb) in enumerate(GROUPS):
                before = GROUPS[g - 1] if g else (0, 0)
                todo = [(m, c) for m in range(before[0], sum(before)) for c in range(LC)]
                for blk in range(NBLK):
                    if g * NBLK + blk >= 2:
                        dve.wait_ge(c_used, g * NBLK + blk - 1)
                    pair_block(b0, nb, (g * NBLK + blk) % 2, blk)
                    if blk >= 1:
                        if blk == 1 and g:
                            dve.wait_ge(end_ev, 2 * sum(n for _, n in GROUPS[:g]))
                        for _ in range(-(-len(todo) // (NBLK - blk))):
                            label_chunk(*todo.pop(0))
            dve.wait_ge(end_ev, 2 * NBT)
            with dve.Fori(GROUPS[-1][0], NBT) as m:
                for c in range(LC):
                    label_chunk(m, c)


_ORDER = ["r_x", "r_label_embedding"] + ["L0_rec_" + n for n in
          ("w1", "b1", "w2", "w3", "b3", "w4", "w5", "b5", "w6", "b6", "w7", "b7", "w8", "b8", "v")]


def kernel(**inputs):
    import numpy as np
    import concourse.bacc as bacc
    from concourse.bass_utils import run_bass_kernel_spmd

    nc = bacc.Bacc("TRN2", target_bir_lowering=False, num_devices=1)
    arrays, args = {}, []
    for name in _ORDER:
        a = np.ascontiguousarray(inputs[name])
        arrays[f"in_{name}"] = a
        args.append(nc.dram_tensor(f"in_{name}", a.shape, mybir.dt.from_np(a.dtype), kind="ExternalInput").ap())
    users, labels = inputs["r_label_embedding"].shape[:2]
    args.append(nc.dram_tensor("scores", (users, labels), F32, kind="ExternalOutput").ap())
    rec_kernel(nc, *args)
    r = run_bass_kernel_spmd(nc, [arrays], core_ids=[0])
    return r.results[0]["scores"]
```

```python
from contextlib import ExitStack

import concourse.bass as bass
from concourse import mybir

F32 = mybir.dt.float32
U32 = mybir.dt.uint32
BF16 = mybir.dt.bfloat16
F32R = mybir.dt.float32r
ALU = mybir.AluOpType
ACT = mybir.ActivationFunctionType
AX = mybir.AxisListType

P = 128
PAD = float(-2 ** 32 + 1)


def rec_kernel(nc, x, label, w1, b1, w2, w3, b3, w4, w5, b5, w6, b6, w7, b7, w8, b8, v, out):
    B, N, E = x.shape
    K = label.shape[1]
    HID = w1.shape[1]
    VC = v.shape[1]
    PAIRS = E * (E - 1) // 2
    NBT = B // P
    CHUNKS = [(c * P, min(P, E - c * P)) for c in range((E + P - 1) // P)]
    NCH = len(CHUNKS)

    UB = P // 2
    T = N // 2
    NS = B // UB
    XSLOTS = 3
    XPRE, XBODY, XLOOPS = 2, 6, 2
    XPOST = NS - XPRE - XBODY * XLOOPS
    HALVES = ((0, (T + 1) // 2), ((T + 1) // 2, T))
    DG, AG = 4, 2
    DGS, AGS = -(-T // DG), -(-T // AG)
    assert DGS % 2 == 1 and AGS % 2 == 1 and XBODY % 6 == 0 and XPRE % 2 == 0
    KB = 13
    BLK = P * KB
    NBLK = (PAIRS + BLK - 1) // BLK
    LASTP = (PAIRS - (NBLK - 1) * BLK) // KB
    assert LASTP * KB == PAIRS - (NBLK - 1) * BLK
    TB = 3
    BODY = 2 * TB
    LOOPS = (NBLK - 1) // BODY
    REST = NBLK - BODY * LOOPS
    assert NBLK % 2 == 1 and NBLK % TB == 0 and REST % 2 == 1
    GROUPS = [(0, 3), (3, 3), (6, 2)]
    NB = max(n for _, n in GROUPS)
    WC = 4
    SPLIT = (3, 2, 1)
    PAIRS_BY = 11
    KNEXT = 10
    LR = 10
    LC = K // LR
    LSLOTS = 5
    assert LC % LSLOTS == 0

    row_start = [i * (E - 1) - i * (i - 1) // 2 for i in range(E)]

    ctx = ExitStack()
    with ctx:
        def sb(name, shape, dt=F32):
            return ctx.enter_context(nc.sbuf_tensor(name, shape, dt))

        def sem(name):
            return ctx.enter_context(nc.semaphore(name))

        stream = sb("stream", [P, 2 * T * E])
        w7ring = sb("w7ring", [P, 2 * KB * E])
        cross = sb("cross", [P, 2 * NB * BLK])
        xslot = [stream[:, 0:T * E], stream[:, T * E:2 * T * E], w7ring[:, 0:T * E]]
        xslot = [a.rearrange("p (t e) -> p t e", e=E) for a in xslot]
        lslot = [stream[:, k * LR * E:(k + 1) * LR * E].rearrange("p (r e) -> p r e", e=E)
                 for k in range(LSLOTS)]
        w7blk = [w7ring[:, k * KB * E:(k + 1) * KB * E] for k in range(2)]
        cblk = [cross[:, k * NB * BLK:(k + 1) * NB * BLK].rearrange("p (b c) -> p b c", c=BLK)
                for k in range(2)]
        at = [0]

        def take(cols, end):
            at[0] += cols
            assert at[0] <= end
            return cross[:, at[0] - cols:at[0]]

        def weights_half(h, end):
            n = HALVES[h][1] - HALVES[h][0]
            return take(n * P, end).rearrange("p (t h b) -> p t h b", t=n, h=2)

        weights = [weights_half(0, NB * BLK)]
        gram = take(NCH * E, NB * BLK).rearrange("p (c e) -> p c e", e=E)
        products = take(DG * E, NB * BLK).bitcast(BF16).rearrange("p (a r e) -> p a r e", a=2, r=DG)
        absum = take(XSLOTS * T, NB * BLK).rearrange("p (k t) -> p k t", t=T)
        masked = take(XSLOTS * T, NB * BLK).rearrange("p (k t) -> p k t", t=T)
        w1nat = take(2 * NCH * HID, NB * BLK).rearrange("p (h c n) -> p h c n", h=2, c=NCH)
        vnat = take(NCH * VC, NB * BLK).rearrange("p (c n) -> p c n", c=NCH)
        w2bc = take(2 * P, NB * BLK)[0:HID, :].rearrange("p (h b) -> p h b", h=2)
        at[0] = NB * BLK
        weights.append(weights_half(1, 2 * NB * BLK))
        w5sb = take(2 * NCH * E, 2 * NB * BLK).rearrange("p (c e) -> p c e", e=E)
        w6sb = take(NCH * E, 2 * NB * BLK).rearrange("p (c e) -> p c e", e=E)
        ubc = take(2 * (E + 1), 2 * NB * BLK).rearrange("p (h e) -> p h e", h=2)
        onehot = take(UB, 2 * NB * BLK)

        cT = [sb(f"cT{k}", [P, NB * P]) for k in range(TB)]
        cHL = [sb(f"cHL{k}", [P, 2, NB * P], F32R) for k in range(TB)]
        wHL = [sb(f"wHL{k}", [P, 2, WC * E], F32R) for k in range(2)]
        score = sb("score", [P, NB, K])
        w8sb = sb("w8sb", [P, 2 * NCH, E])
        h_all = sb("h_all", [P, NBT, E])
        out8 = sb("out8", [P, NBT, E])
        gcol = sb("gcol", [P, NBLK, KB])
        ident = sb("ident", [P, P])
        ones = sb("ones", [P, P])
        brow = sb("brow", [P, E])
        padv = sb("padv", [P, 1])
        tick = sb("tick", [P, 1])
        turnT = sb("turnT", [P, NCH, 2, P])
        turn1 = turnT[:].rearrange("p c h b -> p (c h b)")[:, 0:NCH * P].rearrange("p (c b) -> p c b", c=NCH)
        flat = sb("flat", [P, max(NB, 4), E])
        small = sb("small", [P, XSLOTS, 2, 3 * T + 8])
        w1T = flat[0:HID, 0:3, :].rearrange("p a e -> p (a e)")[:, 0:2 * (E + 1)].rearrange(
            "p (h e) -> p h e", h=2)
        vT = products[0:VC].rearrange("p a b e -> p (a b e)")[:, 0:2 * E].bitcast(F32)
        w2sb = sb("w2sb", [HID, 2])
        gflat = nc.dram_tensor("g_flat", [1, PAIRS], F32, kind="Internal").ap()

        dots = [small[:, k, :, 0:T] for k in range(XSLOTS)]
        expo = [small[:, k, :, T:2 * T] for k in range(XSLOTS)]
        prob = [small[:, k, :, 2 * T:3 * T] for k in range(XSLOTS)]
        maxi = [small[:, k, :, 3 * T:3 * T + 1] for k in range(XSLOTS)]
        maxo = [small[:, k, :, 3 * T + 1:3 * T + 2] for k in range(XSLOTS)]
        nmax = [small[:, k, :, 3 * T + 2:3 * T + 3] for k in range(XSLOTS)]
        part = [small[:, k, :, 3 * T + 3:3 * T + 4] for k in range(XSLOTS)]
        parto = [small[:, k, :, 3 * T + 4:3 * T + 5] for k in range(XSLOTS)]
        total = [small[:, k, :, 3 * T + 5:3 * T + 6] for k in range(XSLOTS)]
        recip = [small[:, k, :, 3 * T + 6:3 * T + 7] for k in range(XSLOTS)]

        bank = [ctx.enter_context(nc.psum_tensor(f"bank{k}", [P, 512], F32)) for k in range(8)]
        acc = bank[0:NB]
        turned = bank[3:3 + TB]
        side = bank[6:8]
        absolutes = bank[2:6]

        small_in = sem("small_in")
        w_in = sem("w_in")
        consts = sem("consts")
        vconsts = sem("vconsts")
        set_mm = sem("set_mm")
        set_ev = sem("set_ev")
        g_stored = sem("g_stored")
        g_in = sem("g_in")
        x_in = [sem(f"x_in{k}") for k in range(XSLOTS)]
        half_used = sem("half_used")
        dots_done = sem("dots_done")
        abs_done = sem("abs_done")
        exp_done = sem("exp_done")
        max_done = sem("max_done")
        prob_raw = sem("prob_raw")
        prob_done = sem("prob_done")
        weights_done = sem("weights_done")
        pool_out = sem("pool_out")
        chain_mm = sem("chain_mm")
        chain_ev = sem("chain_ev")
        link = sem("link")
        c_ready = sem("c_ready")
        c_used = sem("c_used")
        w7_in = [sem(f"w7_in{k}") for k in range(2)]
        w7_used = sem("w7_used")
        turned_done = sem("turned_done")
        cT_done = sem("cT_done")
        cL_done = sem("cL_done")
        wH_done = sem("wH_done")
        wL_done = sem("wL_done")
        split_used = sem("split_used")
        acc_done = sem("acc_done")
        f7_out = sem("f7_out")
        end_mm = sem("end_mm")
        end_ev = sem("end_ev")
        l_in = [sem(f"l_in{k}") for k in range(LSLOTS)]
        l_used = sem("l_used")
        out_stored = sem("out_stored")

        STEPS = (1, 6)
        CH_BT = sum(STEPS)
        SMALL_LOADS = 3 * 2 + 2 + 2
        W_LOADS = 5 * 2 + 4

        def at_tile(t, m):
            return t[:, m, :] if isinstance(m, int) else t[:, bass.ds(m, 1), :].rearrange("p o e -> p (o e)")

        x_v = x.rearrange("(s b) (f t) e -> s (b f) (t e)", b=UB, f=2)
        label_v = label.rearrange("(m p) (c r) e -> m p c (r e)", p=P, r=LR)
        out_v = out.rearrange("(m p) k -> m p k", p=P)
        row = lambda a: a.rearrange("(o e) -> o e", o=1)
        col = lambda a: a.rearrange("(e o) -> e o", o=1)

        class Tile:
            def __init__(self, i, k):
                self.i, self.k = i, k
                self.n = i * XBODY + k
                self.slot, self.half = k % XSLOTS, k % 2
                self.m = i * (XBODY // 2) + k // 2
                self.landed = (i * (XBODY // XSLOTS) + (k // XSLOTS + 1)) * 16
                self.first = isinstance(i, int) and k == 0

            def prev(self, d):
                return Tile(self.i, self.k - d)

        def pooling_tiles(eng):
            for k in range(XPRE):
                yield Tile(0, k)
            with eng.Fori(0, XLOOPS) as i:
                for k in range(XPRE, XPRE + XBODY):
                    yield Tile(i, k)
            for k in range(NS - XPOST, NS):
                yield Tile(0, k)

        def split_chunk(g, k):
            return k // WC if k // WC < SPLIT[g] else None

        chunks0 = [NBLK * sum(SPLIT[:g]) for g in range(len(GROUPS))]

        block = ctx.enter_context(nc.Block())

        @block.sync
        def _(sp):
            def rows_in(dst, src, s):
                full = E // P
                sp.dma_start(dst[:, 0:full, :], src[0:full * P, :].rearrange("(c p) n -> p c n", p=P)).then_inc(s, 16)
                sp.dma_start(dst[0:E - full * P, full, :], src[full * P:E, :]).then_inc(s, 16)

            rows_in(w1nat[:, 0], w1, small_in)
            rows_in(w1nat[:, 1], w3, small_in)
            rows_in(vnat, v, small_in)
            sp.dma_start(w2sb[:, 0:1], w2).then_inc(small_in, 16)
            sp.dma_start(w2sb[:, 1:2], w4).then_inc(small_in, 16)
            sp.dma_start(w1T[:, 0, E:E + 1], col(b1)).then_inc(small_in, 16)
            sp.dma_start(w1T[:, 1, E:E + 1], col(b3)).then_inc(small_in, 16)
            for n in range(XSLOTS):
                sp.dma_start(xslot[n], x_v[n]).then_inc(x_in[n], 16)
            rows_in(w5sb[:, 0:NCH], w5[0:E, :], w_in)
            rows_in(w5sb[:, NCH:2 * NCH], w5[E:2 * E, :], w_in)
            rows_in(w6sb, w6, w_in)
            rows_in(w8sb[:, 0:NCH], w8[0:E, :], w_in)
            rows_in(w8sb[:, NCH:2 * NCH], w8[E:2 * E, :], w_in)
            for k, b in enumerate((b5, b6, b8, b7)):
                sp.dma_start(brow[32 * k:32 * k + 1, :], row(b)).then_inc(w_in, 16)

            sp.wait_ge(set_ev, 5 + NCH)
            share = -(-(E - 1) // (NS - XSLOTS))
            for n in range(XSLOTS, NS):
                sp.wait_ge(half_used, 2 * (n - XSLOTS + 1))
                sp.dma_start(xslot[n % XSLOTS], x_v[n]).then_inc(x_in[n % XSLOTS], 16)
                for i in range((n - XSLOTS) * share, min((n - XSLOTS + 1) * share, E - 1)):
                    sp.dma_start(gflat[:, row_start[i]:row_start[i + 1]],
                                 gram[i % P:i % P + 1, i // P, i + 1:E]).then_inc(g_stored, 16)

            sp.wait_ge(g_stored, 16 * (E - 1))
            sp.wait_ge(consts, 1)
            full = (NBLK - 1) * BLK
            sp.dma_start(gcol[:, 0:NBLK - 1, :],
                         gflat[:, 0:full].rearrange("o (n p k) -> p (o n) k", p=P, k=KB)).then_inc(g_in, 16)
            sp.dma_start(gcol[0:LASTP, NBLK - 1, :],
                         gflat[:, full:PAIRS].rearrange("o (p k) -> (o p) k", k=KB)).then_inc(g_in, 16)

            sp.wait_ge(half_used, 2 * NS)
            for c in range(LSLOTS):
                sp.dma_start(lslot[c], label_v[0, :, c]).then_inc(l_in[c], 16)
            for c in range(LSLOTS, LC):
                sp.wait_ge(l_used, c - LSLOTS + 1)
                sp.dma_start(lslot[c % LSLOTS], label_v[0, :, c]).then_inc(l_in[c % LSLOTS], 16)
            with sp.Fori(1, NBT) as m:
                for c in range(LC):
                    sp.wait_ge(l_used, m * LC + (c - LSLOTS + 1))
                    sp.dma_start(lslot[c % LSLOTS], label_v[bass.ds(m, 1), :, c].rearrange("o p c -> (o p) c")
                                 ).then_inc(l_in[c % LSLOTS], 16)

        @block.gpsimd
        def _(pool):
            ki = [0]

            def step(ins):
                ki[0] += 1
                ins.then_inc(consts, 1)
                pool.wait_ge(consts, ki[0])

            step(nc.gpsimd.memset(gcol[:], 0.0))
            step(nc.gpsimd.memset(ident[:], 0.0))
            step(nc.gpsimd.memset(onehot, 0.0))
            step(nc.gpsimd.affine_select(out=ident[:], in_=ident[:], compare_op=ALU.not_equal, fill=1.0,
                                         base=0, pattern=[[-1, P]], channel_multiplier=1))
            for f in range(2):
                step(nc.gpsimd.affine_select(out=onehot, in_=onehot, compare_op=ALU.not_equal,
                                             fill=1.0, base=-f, pattern=[[-2, UB]], channel_multiplier=1))

            for tile in pooling_tiles(pool):
                pool.wait_ge(prob_done, tile.n + 1)
                for h, (t0, t1) in enumerate(HALVES):
                    if not tile.first:
                        pool.wait_ge(half_used, tile.n * 2 + (h - 1))
                    nc.gpsimd.tensor_tensor(
                        weights[h],
                        prob[tile.slot][:, :, t0:t1].rearrange("p h t -> p t h").unsqueeze(3).to_broadcast(
                            [P, t1 - t0, 2, UB]),
                        onehot.unsqueeze(1).unsqueeze(1).to_broadcast([P, t1 - t0, 2, UB]),
                        ALU.mult).then_inc(weights_done, 1)

            for m in range(NBT):
                j = next(m - b0 for b0, nb in GROUPS if m < b0 + nb)
                pool.wait_ge(l_used, (m + 1) * LC)
                pool.dma_start(out_v[m], score[:, j, :]).then_inc(out_stored, 16)
            pool.wait_ge(out_stored, 16 * NBT)

        @block.tensor
        def _(pe):
            pe.wait_ge(consts, 6)
            pe.wait_ge(small_in, 16 * SMALL_LOADS)
            for hd in range(2):
                for c, (o, n) in enumerate(CHUNKS):
                    mm = pe.transpose(bank[2 + hd][0:HID, o:o + n], w1nat[0:n, hd, c, :], ident[0:n, 0:n])
                mm.then_inc(set_mm, 1)
            for c, (o, n) in enumerate(CHUNKS):
                mm = pe.transpose(bank[4][0:VC, o:o + n], vnat[0:n, c, :], ident[0:n, 0:n])
            mm.then_inc(set_mm, 1)
            pe.wait_ge(set_ev, 3)
            pe.wait_ge(vconsts, 3)
            for hd in range(2):
                pe.matmul(bank[6 + hd][:, 0:E + 1], w2bc[:, hd, :], w1T[:, hd, :],
                          start=True, stop=True).then_inc(set_mm, 1)
            for c, (o, n) in enumerate(CHUNKS):
                pe.matmul(bank[2 + c][0:n, 0:E], vT[:, o:o + n], vT, start=True, stop=True).then_inc(set_mm, 1)

            def tturn(dst, src):
                for c, (o, n) in enumerate(CHUNKS):
                    mm = pe.transpose(dst[0:n, c * P:(c + 1) * P], src[:, o:o + n], ident[:])
                return mm

            def spread_row(dst, k):
                o = 32 * k
                return pe.matmul(dst[:, 0:E], ones[o:o + 1, :], brow[o:o + 1, :], start=True, stop=False)

            def rows_mm(dst, lhs, rhs, bias, nlhs):
                mm = spread_row(dst, bias)
                for q in range(nlhs):
                    n = CHUNKS[q % NCH][1]
                    mm = pe.matmul(dst[:, 0:E], lhs(q)[0:n, :], rhs[0:n, q, :], start=False, stop=(q == nlhs - 1))
                return mm

            def chain(m, s, step):
                if step == 0:
                    pe.wait_ge(pool_out, m * 2 + s + 1)
                pe.wait_ge(chain_ev, m * CH_BT + s + step)
                dst = side[step % 2]
                if step == 0:
                    mm = tturn(dst, flat[:, s, :])
                elif step == 1:
                    mm = rows_mm(dst, lambda q: turnT[:, q % NCH, q // NCH, :], w5sb, 0, 2 * NCH)
                elif step == 2:
                    mm = tturn(dst, flat[:, 3, :])
                elif step == 3:
                    mm = rows_mm(dst, lambda q: turn1[:, q, :], w6sb, 1, NCH)
                elif step == 4:
                    mm = tturn(dst, flat[:, 2, :])
                else:
                    mm = rows_mm(dst, lambda q: turn1[:, q, :], w8sb, 2, NCH)
                mm.then_inc(chain_mm, 1)

            pe.wait_ge(w_in, 16 * W_LOADS)
            pe.wait_ge(set_ev, 5 + NCH)
            for tile in pooling_tiles(pe):
                last = tile.prev(1)
                steps = [] if tile.first else list(range(STEPS[last.half]))
                for h, (t0, t1) in enumerate(HALVES):
                    if steps:
                        chain(last.m, last.half, steps.pop(0))
                    pe.wait_ge(weights_done, tile.n * 2 + (h + 1))
                    for t in range(t0, t1):
                        mm = pe.matmul(bank[tile.half][:, 0:E], weights[h][:, t - t0],
                                       xslot[tile.slot][:, t, :], start=(t == 0), stop=(t == T - 1))
                        if t % 4 == 3 and steps and t + 1 < t1:
                            chain(last.m, last.half, steps.pop(0))
                    mm.then_inc(half_used, 1)
                assert not steps
            for step in range(STEPS[1]):
                chain(NBT - 1, 1, step)

            loads = [0, 0]
            for g, (b0, nb) in enumerate(GROUPS):
                blk0, tile0 = g * NBLK, g * NBLK * KB

                def turn(blk, k):
                    if k == 0:
                        pe.wait_ge(c_ready, blk[0] + (blk0 + blk[1] + 1))
                    q = (tile0 + blk[1] * KB + k) % TB
                    for b in range(nb):
                        mm = pe.transpose(turned[q][:, b * P:(b + 1) * P],
                                          cblk[(blk0 + blk[1]) % 2][:, b, k:BLK:KB], ident[:])
                    mm.then_inc(turned_done, 1)

                def contract(blk, i, k, landed, np_):
                    slot, q = (blk0 + blk) % 2, (tile0 + blk * KB + k) % TB
                    last = blk == NBLK - 1 and k == KB - 1
                    chunk = split_chunk(g, k)
                    if k == 0:
                        pe.wait_ge(w7_in[slot], landed)
                    if chunk is not None and k % WC == 0:
                        pe.wait_ge(wL_done, i * (BODY * SPLIT[g]) + (chunks0[g] + blk * SPLIT[g] + chunk + 1))
                    pe.wait_ge(cT_done, i * (BODY * KB) + (tile0 + blk * KB + k + 1))
                    if chunk is None:
                        passes = [(cT[q], w7blk[slot][:, k * E:(k + 1) * E])]
                    else:
                        wb, r = wHL[(chunks0[g] + blk * SPLIT[g] + chunk) % 2], k % WC
                        wh, wl = wb[:, 0, r * E:(r + 1) * E], wb[:, 1, r * E:(r + 1) * E]
                        passes = [(cHL[q][:, 0], wh), (cHL[q][:, 0], wl), (cHL[q][:, 1], wh)]
                    for j, (lhs, rhs) in enumerate(passes):
                        if j == 2:
                            pe.wait_ge(cL_done, i * (BODY * WC * SPLIT[g])
                                       + (WC * (chunks0[g] + blk * SPLIT[g]) + k + 1))
                        for b in range(nb):
                            mm = pe.matmul(acc[b][:, 0:E], lhs[0:np_, b * P:(b + 1) * P], rhs[0:np_, :],
                                           start=False, stop=last and j == len(passes) - 1)
                            if k == KB - 3 and j == 0 and b == 0:
                                mm.then_inc(c_used, 1)
                    if last:
                        mm.then_inc(acc_done, 1)
                    elif k == KB - 1:
                        mm.then_inc(w7_used, 1)
                    elif chunk is not None and k % WC == WC - 1:
                        mm.then_inc(split_used, 1)

                if g == 0:
                    pe.wait_ge(chain_ev, CH_BT * NBT)
                else:
                    pe.wait_ge(f7_out, b0)
                for b in range(nb):
                    mm = spread_row(acc[b], 3)
                    if g == 0 and b == 0:
                        mm.then_inc(split_used, 1)
                    if g == 0 and b == 1:
                        mm.then_inc(w7_used, 1)
                turn((0, 0), 0)
                turn((0, 0), 1)
                s0, s1 = blk0 % 2, (blk0 + 1) % 2

                def tile_step(i, blk, k, landed, np_):
                    ahead = blk * KB + k + 2
                    if not isinstance(i, int) or ahead < NBLK * KB:
                        turn((i * BODY, ahead // KB), ahead % KB)
                    contract(blk, i, k, landed, np_)

                with pe.Fori(0, LOOPS) as i:
                    for blk in range(BODY):
                        for k in range(KB):
                            tile_step(i, blk, k, (i * (BODY // 2) + (loads[(s0, s1)[blk % 2]] + blk // 2 + 1)) * 16, P)
                for blk in range(NBLK - REST, NBLK):
                    slot = (s0, s1)[blk % 2]
                    for k in range(KB):
                        if blk < NBLK - 1:
                            tile_step(0, blk, k, 16 * (loads[slot] + blk // 2 + 1), P)
                        else:
                            tile_step(0, blk, k, 16 * (loads[slot] + blk // 2 + 2), LASTP)
                loads[s0] += NBLK // 2 + 2
                loads[s1] += NBLK // 2

                for b in range(nb):
                    e = 2 * (b0 + b)
                    pe.wait_ge(f7_out, b0 + b + 1)
                    if e:
                        pe.wait_ge(end_ev, e)
                    tturn(side[0], flat[:, b, :]).then_inc(end_mm, 1)
                    pe.wait_ge(end_ev, e + 1)
                    pe.matmul(side[1][:, 0:E], ident[:], out8[:, b0 + b, :], start=True, stop=False)
                    for c, (_, n) in enumerate(CHUNKS):
                        mm = pe.matmul(side[1][:, 0:E], turn1[0:n, c, :], w8sb[0:n, NCH + c, :],
                                       start=False, stop=(c == NCH - 1))
                    mm.then_inc(end_mm, 1)

        @block.scalar
        def _(act):
            def cp(dst, src):
                return nc.scalar.activation(dst, src, ACT.Copy)

            def absolute(tile, t):
                grp, r = t // AG, t % AG
                if r == 0 and not (tile.first and grp < 2):
                    act.wait_ge(abs_done, tile.n * AGS + (grp - 1))
                ins = nc.scalar.activation(absolutes[(tile.half + grp) % 2 * AG + r][:, 0:E],
                                           xslot[tile.slot][:, t, :], ACT.Abs,
                                           accum_out=absum[:, tile.slot, t:t + 1])
                if r == AG - 1 or t == T - 1:
                    ins.then_inc(abs_done, 1)

            def exps(tile):
                act.wait_ge(dots_done, (tile.n + 1) * (2 * DGS))
                for hd in range(2):
                    ins = nc.scalar.activation(expo[tile.slot][:, hd, :], dots[tile.slot][:, hd, :], ACT.Exp,
                                               bias=ubc[:, hd, E:E + 1])
                ins.then_inc(exp_done, 1)

            def softexp(tile):
                k = tile.slot
                act.wait_ge(max_done, tile.n + 1)
                for hd in range(2):
                    ins = nc.scalar.activation(prob[k][:, hd, :], expo[k][:, hd, :], ACT.Exp,
                                               bias=nmax[k][:, hd, :], accum_out=part[k][:, hd, :])
                ins.then_inc(prob_raw, 1)

            def turned_out(dst3, src):
                cp(dst3[:, 0:NCH - 1], src[:, 0:(NCH - 1) * P].rearrange("p (c b) -> p c b", b=P))
                n = CHUNKS[-1][1]
                return cp(dst3[0:n, NCH - 1], src[0:n, (NCH - 1) * P:NCH * P])

            def pools_turned(src, s):
                for c, (_, n) in enumerate(CHUNKS):
                    ins = cp(turnT[0:n, c, :, s * UB:(s + 1) * UB],
                             src[0:n, c * P:(c + 1) * P].rearrange("p (h b) -> p h b", h=2))
                return ins

            def chain_out(m, s, step):
                act.wait_ge(chain_mm, m * CH_BT + (s + step + 1))
                src = side[step % 2]
                if step == 0:
                    ins = pools_turned(src, s)
                elif step == 1:
                    cp(at_tile(h_all, m), src[:, 0:E])
                    ins = cp(flat[:, 3, :], src[:, 0:E])
                elif step == 3:
                    ins = cp(flat[:, 2, :], src[:, 0:E])
                elif step == 5:
                    ins = cp(at_tile(out8, m), src[:, 0:E])
                else:
                    ins = turned_out(turn1, src)
                ins.then_inc(chain_ev, 1)

            def pools_out(m, s):
                act.wait_ge(half_used, m * 4 + (2 * s + 2))
                cp(flat[:, s, :], bank[s][:, 0:E]).then_inc(pool_out, 1)

            act.wait_ge(set_ev, 5 + NCH)
            for tile in pooling_tiles(act):
                before = [] if tile.first else [tile.prev(1)]
                chains = []
                if before:
                    exps(before[0])
                if before and not before[0].first:
                    done = tile.prev(2)
                    chains = [(done.m, done.half, step) for step in range(STEPS[done.half])]
                act.wait_ge(x_in[tile.slot], tile.landed)
                for t in range(T):
                    absolute(tile, t)
                    if t == 4 and before:
                        softexp(before[0])
                    if t == 5 and chains:
                        pools_out(done.m, done.half)
                    if t > 12 and t % 2 == 1 and chains:
                        chain_out(*chains.pop(0))
                assert not chains
            exps(Tile(0, NS - 1))
            softexp(Tile(0, NS - 1))
            pools_out(NBT - 1, 0)
            chain_out(NBT - 1, 0, 0)
            pools_out(NBT - 1, 1)
            for step in range(STEPS[1]):
                chain_out(NBT - 1, 1, step)

            act.wait_ge(g_in, 32)
            full = (NBLK - 1) * BLK
            w7_v = w7[0:full, :].rearrange("(n p k) e -> n p (k e)", p=P, k=KB)
            w7_last = w7[full:PAIRS, :].rearrange("(p k) e -> p (k e)", k=KB)

            def load(slot, blk):
                act.dma_start(w7blk[slot], w7_v[blk] if isinstance(blk, int) else
                              w7_v[bass.ds(blk, 1)].rearrange("o p c -> (o p) c")).then_inc(w7_in[slot], 16)

            def load_last(slot):
                cut = LASTP // 16 * 16
                act.dma_start(w7blk[slot][0:cut], w7_last[0:cut]).then_inc(w7_in[slot], 16)
                act.dma_start(w7blk[slot][cut:LASTP], w7_last[cut:LASTP]).then_inc(w7_in[slot], 16)

            act.wait_ge(half_used, 2 * NS)
            load(0, 0)
            loads = [0, 0]
            for g, (b0, nb) in enumerate(GROUPS):
                blk0, tile0, used = g * NBLK, g * NBLK * KB, g * (NBLK - 1)
                s0, s1 = blk0 % 2, (blk0 + 1) % 2

                def scaled(tiles, blk, k, gblk, np_):
                    act.wait_ge(turned_done, tiles + (tile0 + blk * KB + k + 1))
                    q = (tile0 + blk * KB + k) % TB
                    dst = cT[q] if split_chunk(g, k) is None else cHL[q][:, 0]
                    nc.scalar.activation(dst[0:np_, 0:nb * P], turned[q][0:np_, 0:nb * P], ACT.Copy,
                                         scale=gblk[0:np_, k:k + 1]).then_inc(cT_done, 1)

                def w7_high(i, blk, chunk, landed, np_=P):
                    c = chunks0[g] + blk * SPLIT[g] + chunk
                    if chunk == 0:
                        act.wait_ge(w7_in[(blk0 + blk) % 2], landed)
                    if c > 0:
                        act.wait_ge(split_used, i * (BODY * SPLIT[g]) + c)
                    nc.scalar.activation(wHL[c % 2][0:np_, 0, :],
                                         w7blk[(blk0 + blk) % 2][0:np_, chunk * WC * E:(chunk + 1) * WC * E],
                                         ACT.Copy).then_inc(wH_done, 1)

                def w7_highs(i, blk, k, landed, np_=P, np_next=P):
                    if k % WC == 1 and k // WC + 1 < SPLIT[g]:
                        w7_high(i, blk, k // WC + 1, None, np_)
                    if k == KNEXT and landed is not None:
                        w7_high(i, blk + 1, 0, landed, np_next)

                l0, l1 = 16 * loads[s0], 16 * loads[s1]
                w7_high(0, 0, 0, l0 + 16)

                with act.Fori(0, LOOPS) as i:
                    for blk in range(BODY):
                        for k in range(KB):
                            scaled(i * (BODY * KB), blk, k, at_tile(gcol, i * BODY + blk), P)
                            nxt = blk + 1
                            w7_highs(i, blk, k, (i * (BODY // 2) + (nxt // 2 + 1)) * 16 + (l0, l1)[nxt % 2])
                            if k == 2:
                                act.wait_ge(w7_used, i * BODY + (used + blk + 1))
                                load((s0, s1)[nxt % 2], i * BODY + nxt)
                for blk in range(NBLK - REST, NBLK):
                    for k in range(KB):
                        scaled(0, blk, k, gcol[:, blk, :], P if blk < NBLK - 1 else LASTP)
                        nxt = blk + 1
                        landed = (l0, l1)[nxt % 2] + 16 * (nxt // 2 + (1 if nxt < NBLK - 1 else 2))
                        w7_highs(0, blk, k, landed if nxt < NBLK else None,
                                 P if blk < NBLK - 1 else LASTP, P if blk < NBLK - 2 else LASTP)
                        if k == 2:
                            act.wait_ge(w7_used, used + blk + 1)
                            if nxt < NBLK - 1:
                                load((s0, s1)[nxt % 2], nxt)
                            elif nxt == NBLK - 1:
                                load_last(s0)
                            elif g + 1 < len(GROUPS):
                                load(s1, 0)

                loads[s0] += NBLK // 2 + 2
                loads[s1] += NBLK // 2

                act.wait_ge(acc_done, g + 1)
                for b in range(nb):
                    cp(flat[:, b, :], acc[b][:, 0:E]).then_inc(f7_out, 1)
                for b in range(nb):
                    e = 2 * (b0 + b)
                    act.wait_ge(end_mm, e + 1)
                    turned_out(turn1, side[0]).then_inc(end_ev, 1)
                    act.wait_ge(end_mm, e + 2)
                    cp(out8[:, b0 + b, :], side[1][:, 0:E]).then_inc(end_ev, 1)

        @block.vector
        def _(dve):
            nc.vector.memset(ones[:], 1.0).then_inc(vconsts, 1)
            nc.vector.memset(padv[:], PAD).then_inc(vconsts, 1)
            dve.wait_ge(small_in, 16 * SMALL_LOADS)
            nc.vector.tensor_copy(w2bc, w2sb[:].unsqueeze(2).to_broadcast([HID, 2, P])).then_inc(vconsts, 1)
            for hd in range(2):
                dve.wait_ge(set_mm, hd + 1)
                nc.vector.tensor_copy(w1T[:, hd, 0:E], bank[2 + hd][0:HID, 0:E]).then_inc(set_ev, 1)
            dve.wait_ge(set_mm, 3)
            nc.vector.tensor_copy(vT, bank[4][0:VC, 0:E]).then_inc(set_ev, 1)
            for hd in range(2):
                dve.wait_ge(set_mm, 4 + hd)
                nc.vector.tensor_copy(ubc[:, hd, :], bank[6 + hd][:, 0:E + 1]).then_inc(set_ev, 1)
            for c, (o, n) in enumerate(CHUNKS):
                dve.wait_ge(set_mm, 6 + c)
                nc.vector.tensor_copy(gram[0:n, c, :], bank[2 + c][0:n, 0:E]).then_inc(set_ev, 1)
            dve.wait_ge(set_ev, 5 + NCH)

            SWAP = [q ^ 1 for q in range(32)]

            def score_row(tile, q):
                hd, t = q // T, q % T
                grp, r = hd * DGS + t // DG, t % DG
                if r == 0 and not (tile.first and grp < 2):
                    dve.wait_ge(dots_done, tile.n * (2 * DGS) + (grp - 1))
                ins = nc.vector.scalar_tensor_tensor(
                    out=products[:, grp % 2, r, :], in0=xslot[tile.slot][:, t, :], scalar=1.0,
                    in1=ubc[:, hd, 0:E], op0=ALU.mult, op1=ALU.mult,
                    accum_out=dots[tile.slot][:, hd, t:t + 1])
                if r == DG - 1 or t == T - 1:
                    ins.then_inc(dots_done, 1)

            LINKS = 8

            def linked(ins, n, j):
                ins.then_inc(link, 1)
                dve.wait_ge(link, n * LINKS + j)

            def carry():
                nc.vector.memset(tick[:], 0.0)

            def maxima(n, k):
                dve.wait_ge(exp_done, n + 1)
                dve.wait_ge(abs_done, (n + 1) * AGS)
                linked(nc.vector.tensor_scalar(masked[:, k, :], absum[:, k, :], 0.0, None, ALU.is_equal), n, 1)
                carry()
                for hd in range(2):
                    ins = nc.vector.copy_predicated(expo[k][:, hd, :], masked[:, k, :].bitcast(U32),
                                                    padv[:].to_broadcast([P, T]))
                linked(ins, n, 2)
                linked(nc.vector.tensor_reduce(maxi[k], expo[k], AX.X, ALU.max), n, 3)
                carry()
                linked(nc.vector.stream_shuffle(maxo[k], maxi[k], SWAP), n, 4)
                linked(nc.vector.tensor_tensor(maxi[k], maxi[k], maxo[k], ALU.max), n, 5)
                nc.vector.tensor_scalar(nmax[k], maxi[k], -1.0, None, ALU.mult).then_inc(max_done, 1)

            def normalise(n, k):
                dve.wait_ge(prob_raw, n + 1)
                carry()
                linked(nc.vector.stream_shuffle(parto[k], part[k], SWAP), n, 6)
                linked(nc.vector.tensor_tensor(total[k], part[k], parto[k], ALU.add), n, 7)
                linked(nc.vector.reciprocal(recip[k], total[k]), n, 8)
                nc.vector.tensor_tensor(prob[k], prob[k], recip[k].to_broadcast([P, 2, T]),
                                        ALU.mult).then_inc(prob_done, 1)

            for tile in pooling_tiles(dve):
                dve.wait_ge(x_in[tile.slot], tile.landed)
                for q in range(2 * T):
                    score_row(tile, q)
                    if not tile.first and q == 7:
                        maxima(tile.prev(1).n, tile.prev(1).slot)
                    if not tile.first and q == 17:
                        normalise(tile.prev(1).n, tile.prev(1).slot)
            maxima(NS - 1, (NS - 1) % XSLOTS)
            normalise(NS - 1, (NS - 1) % XSLOTS)

            def label_row(m, j, q):
                c, r = q // LR, q % LR
                row_in = lslot[c % LSLOTS][:, r, :]
                if r == 0:
                    dve.wait_ge(l_in[c % LSLOTS], m * (16 * LC // LSLOTS) + 16 * (c // LSLOTS + 1))
                ins = nc.vector.scalar_tensor_tensor(
                    out=row_in, in0=row_in, scalar=1.0, in1=out8[:, m, :], op0=ALU.mult, op1=ALU.mult,
                    accum_out=score[:, j, q:q + 1])
                if r == LR - 1:
                    ins.then_inc(l_used, 1)

            def rows_of(blk):
                lo, hi = blk * BLK, min((blk + 1) * BLK, PAIRS)
                return [(i, max(lo, row_start[i]), min(hi, row_start[i + 1])) for i in range(E - 1)
                        if max(lo, row_start[i]) < min(hi, row_start[i + 1])]

            def pair_row(g, blk, r):
                b0, nb = GROUPS[g]
                gblk, rows = g * NBLK + blk, rows_of(blk)
                i, a, z = rows[r]
                j, n = i + 1 + a - row_start[i], z - a
                if r == 0 and gblk >= 2:
                    dve.wait_ge(c_used, gblk - 1)
                dst = cblk[gblk % 2][:, 0:nb, a - blk * BLK:z - blk * BLK]
                if nb * (60 + n / 2) < 60 + nb * n:
                    for b in range(nb):
                        ins = nc.vector.tensor_scalar(dst[:, b], h_all[:, b0 + b, j:j + n],
                                                      h_all[:, b0 + b, i:i + 1], None, ALU.mult)
                else:
                    ins = nc.vector.tensor_tensor(dst, h_all[:, b0:b0 + nb, j:j + n],
                                                  h_all[:, b0:b0 + nb, i:i + 1].to_broadcast([P, nb, n]),
                                                  ALU.mult)
                if r == len(rows) - 1:
                    ins.then_inc(c_ready, 1)

            def w7_low(g, blk, chunk, np_):
                c = chunks0[g] + blk * SPLIT[g] + chunk
                dve.wait_ge(wH_done, c + 1)
                wb = wHL[c % 2]
                nc.vector.tensor_tensor(wb[0:np_, 1, :],
                                        w7blk[(g * NBLK + blk) % 2][0:np_, chunk * WC * E:(chunk + 1) * WC * E],
                                        wb[0:np_, 0, :].bitcast(F32), ALU.subtract).then_inc(wL_done, 1)

            def cross_low(g, blk, k, np_):
                nb = GROUPS[g][1]
                t = g * NBLK * KB + blk * KB + k
                dve.wait_ge(cT_done, t + 1)
                nc.vector.scalar_tensor_tensor(
                    out=cHL[t % TB][0:np_, 1, 0:nb * P], in0=turned[t % TB][0:np_, 0:nb * P],
                    scalar=gcol[0:np_, blk, k:k + 1], in1=cHL[t % TB][0:np_, 0, 0:nb * P].bitcast(F32),
                    op0=ALU.mult, op1=ALU.subtract).then_inc(cL_done, 1)

            dve.wait_ge(g_stored, 16 * (E - 1))
            dve.wait_ge(half_used, 2 * NS - 1)
            for r in range(len(rows_of(0))):
                pair_row(0, 0, r)
            dve.wait_ge(chain_ev, CH_BT * NBT)
            dve.wait_ge(g_in, 32)
            for g in range(len(GROUPS)):
                p0, pn = GROUPS[g - 1] if g else (0, 0)
                labels = pn * K
                w7_low(g, 0, 0, P)
                for blk in range(NBLK):
                    np_ = P if blk < NBLK - 1 else LASTP
                    g1, blk1 = (g, blk + 1) if blk + 1 < NBLK else (g + 1, 0)
                    rows1 = len(rows_of(blk1)) if g1 < len(GROUPS) else 0
                    if blk == 1 and g:
                        dve.wait_ge(end_ev, 2 * (p0 + pn))
                        if p0:
                            dve.wait_ge(out_stored, 16 * p0)
                    for k in range(KB):
                        if split_chunk(g, k) is not None:
                            cross_low(g, blk, k, np_)
                        if k % WC == 1 and k // WC + 1 < SPLIT[g]:
                            w7_low(g, blk, k // WC + 1, np_)
                        if k == KNEXT and blk + 1 < NBLK:
                            w7_low(g, blk + 1, 0, P if blk + 2 < NBLK else LASTP)
                        for r in range(rows1 * min(k, PAIRS_BY) // PAIRS_BY,
                                       rows1 * min(k + 1, PAIRS_BY) // PAIRS_BY):
                            pair_row(g1, blk1, r)
                        first, tiles = KB, (NBLK - 1) * KB
                        t = blk * KB + k - first
                        if t >= 0:
                            for q in range(labels * t // tiles, labels * (t + 1) // tiles):
                                label_row(p0 + q // K, q // K, q % K)

            p0, pn = GROUPS[-1]
            dve.wait_ge(end_ev, 2 * (p0 + pn))
            dve.wait_ge(out_stored, 16 * p0)
            for j in range(pn):
                for q in range(K):
                    label_row(p0 + j, j, q)


_ORDER = ["r_x", "r_label_embedding"] + ["L0_rec_" + n for n in
          ("w1", "b1", "w2", "w3", "b3", "w4", "w5", "b5", "w6", "b6", "w7", "b7", "w8", "b8", "v")]


def kernel(**inputs):
    import numpy as np
    import concourse.bacc as bacc
    from concourse.bass_utils import run_bass_kernel_spmd

    nc = bacc.Bacc("TRN2", target_bir_lowering=False, num_devices=1)
    arrays, args = {}, []
    for name in _ORDER:
        a = np.ascontiguousarray(inputs[name])
        arrays[f"in_{name}"] = a
        args.append(nc.dram_tensor(f"in_{name}", a.shape, mybir.dt.from_np(a.dtype), kind="ExternalInput").ap())
    users, labels = inputs["r_label_embedding"].shape[:2]
    args.append(nc.dram_tensor("scores", (users, labels), F32, kind="ExternalOutput").ap())
    rec_kernel(nc, *args)
    r = run_bass_kernel_spmd(nc, [arrays], core_ids=[0])
    return r.results[0]["scores"]
```

```python
from contextlib import ExitStack

import concourse.bass as bass
from concourse import mybir

F32 = mybir.dt.float32
U32 = mybir.dt.uint32
BF16 = mybir.dt.bfloat16
F32R = mybir.dt.float32r
ALU = mybir.AluOpType
ACT = mybir.ActivationFunctionType
AX = mybir.AxisListType

P = 128
PAD = float(-2 ** 32 + 1)


def rec_kernel(nc, x, label, w1, b1, w2, w3, b3, w4, w5, b5, w6, b6, w7, b7, w8, b8, v, out):
    B, N, E = x.shape
    K = label.shape[1]
    HID = w1.shape[1]
    VC = v.shape[1]
    PAIRS = E * (E - 1) // 2
    NBT = B // P
    CHUNKS = [(c * P, min(P, E - c * P)) for c in range((E + P - 1) // P)]
    NCH = len(CHUNKS)

    UB = P // 2
    T = N // 2
    NS = B // UB
    XSLOTS = 3
    XPRE, XBODY, XLOOPS = 4, 6, 2
    XPOST = NS - XPRE - XBODY * XLOOPS
    MAX_AT, NORM_AT = 3, 12
    EXP_AT, OUT_AT = 3, 11
    TURN_AT, LATE_AT = 17, 4
    FOLD_AT = 13
    PE_STEPS = (4, 24)
    HALVES = ((0, (T + 1) // 2), ((T + 1) // 2, T))
    DG, AG = 4, 2
    DGS, AGS = -(-T // DG), -(-T // AG)
    assert DGS % 2 == 1 and AGS % 2 == 1 and XBODY % 6 == 0 and XPRE % 2 == 0
    KB = 13
    BLK = P * KB
    NBLK = (PAIRS + BLK - 1) // BLK
    LASTP = (PAIRS - (NBLK - 1) * BLK) // KB
    assert LASTP * KB == PAIRS - (NBLK - 1) * BLK
    TB = 3
    BODY = 2 * TB
    LOOPS = (NBLK - 1) // BODY
    REST = NBLK - BODY * LOOPS
    assert NBLK % 2 == 1 and NBLK % TB == 0 and REST % 2 == 1
    GROUPS = [(0, 3), (3, 3), (6, 2)]
    NB = max(n for _, n in GROUPS)
    WC = 4
    SPLIT = (3, 2, 1)
    PAIRS_BY = 11
    OUT8_BY = 4
    KNEXT = 10
    LR = 10
    LC = K // LR
    LSLOTS = 5
    assert LC % LSLOTS == 0

    row_start = [i * (E - 1) - i * (i - 1) // 2 for i in range(E)]

    ctx = ExitStack()
    with ctx:
        def sb(name, shape, dt=F32):
            return ctx.enter_context(nc.sbuf_tensor(name, shape, dt))

        def sem(name):
            return ctx.enter_context(nc.semaphore(name))

        stream = sb("stream", [P, 2 * T * E])
        w7ring = sb("w7ring", [P, 2 * KB * E])
        cross = sb("cross", [P, 2 * NB * BLK])
        xslot = [stream[:, 0:T * E], stream[:, T * E:2 * T * E], w7ring[:, 0:T * E]]
        xslot = [a.rearrange("p (t e) -> p t e", e=E) for a in xslot]
        lslot = [stream[:, k * LR * E:(k + 1) * LR * E].rearrange("p (r e) -> p r e", e=E)
                 for k in range(LSLOTS)]
        w7blk = [w7ring[:, k * KB * E:(k + 1) * KB * E] for k in range(2)]
        cblk = [cross[:, k * NB * BLK:(k + 1) * NB * BLK].rearrange("p (b c) -> p b c", c=BLK)
                for k in range(2)]
        at = [0]

        def take(cols, end):
            at[0] += cols
            assert at[0] <= end
            return cross[:, at[0] - cols:at[0]]

        def weights_half(h, end):
            n = HALVES[h][1] - HALVES[h][0]
            return take(n * P, end).rearrange("p (t h b) -> p t h b", t=n, h=2)

        weights = [weights_half(0, NB * BLK)]
        gram = take(NCH * E, NB * BLK).rearrange("p (c e) -> p c e", e=E)
        products = take(DG * E, NB * BLK).bitcast(BF16).rearrange("p (a r e) -> p a r e", a=2, r=DG)
        absum = take(XSLOTS * T, NB * BLK).rearrange("p (k t) -> p k t", t=T)
        masked = take(XSLOTS * T, NB * BLK).rearrange("p (k t) -> p k t", t=T)
        w1nat = take(2 * NCH * HID, NB * BLK).rearrange("p (h c n) -> p h c n", h=2, c=NCH)
        vnat = take(NCH * VC, NB * BLK).rearrange("p (c n) -> p c n", c=NCH)
        w2bc = take(2 * P, NB * BLK)[0:HID, :].rearrange("p (h b) -> p h b", h=2)
        at[0] = NB * BLK
        weights.append(weights_half(1, 2 * NB * BLK))
        w5sb = take(2 * NCH * E, 2 * NB * BLK).rearrange("p (c e) -> p c e", e=E)
        ubc = take(2 * (E + 1), 2 * NB * BLK).rearrange("p (h e) -> p h e", h=2)
        onehot = take(UB, 2 * NB * BLK)

        cT = [sb(f"cT{k}", [P, NB * P]) for k in range(TB)]
        cHL = [sb(f"cHL{k}", [P, 2, NB * P], F32R) for k in range(TB)]
        wHL = [sb(f"wHL{k}", [P, 2, WC * E], F32R) for k in range(2)]
        score = sb("score", [P, NB, K])
        w8b = sb("w8b", [P, NCH, E])
        w568 = sb("w568", [P, 2 * NCH, E])
        h_all = sb("h_all", [P, NBT, E])
        out8 = sb("out8", [P, NBT, E])
        setup = out8[:].rearrange("p m e -> p (m e)")
        w6nat, w6T = setup[:, 0:NCH * E], setup[:, NCH * E:2 * NCH * E]
        w5T = setup[:, 0:2 * NCH * E].rearrange("p (h c e) -> p h c e", h=2, c=NCH)
        w6nat, w6T = (a.rearrange("p (c e) -> p c e", e=E) for a in (w6nat, w6T))
        w8a = h_all[:, 0:NCH, :]
        w68 = h_all[:, NCH:2 * NCH, :]
        bcol = sb("bcol", [P, 2, NCH])
        gcol = sb("gcol", [P, NBLK, KB])
        ident = sb("ident", [P, P])
        ones = sb("ones", [P, P])
        brow = sb("brow", [P, E])
        B_OUT, B5, B8, B7 = range(4)
        padv = sb("padv", [P, 1])
        tick = sb("tick", [P, 1])
        turnT = sb("turnT", [P, NCH, 2, P])
        turn1 = turnT[:].rearrange("p c h b -> p (c h b)")[:, 0:NCH * P].rearrange("p (c b) -> p c b", c=NCH)
        flat = sb("flat", [P, NB, E])
        small = sb("small", [P, XSLOTS, 2, 3 * T + 8])
        w1T = flat[0:HID, 0:3, :].rearrange("p a e -> p (a e)")[:, 0:2 * (E + 1)].rearrange(
            "p (h e) -> p h e", h=2)
        vT = products[0:VC].rearrange("p a b e -> p (a b e)")[:, 0:2 * E].bitcast(F32)
        w2sb = sb("w2sb", [HID, 2])
        gflat = nc.dram_tensor("g_flat", [1, PAIRS], F32, kind="Internal").ap()

        dots = [small[:, k, :, 0:T] for k in range(XSLOTS)]
        expo = [small[:, k, :, T:2 * T] for k in range(XSLOTS)]
        prob = [small[:, k, :, 2 * T:3 * T] for k in range(XSLOTS)]
        maxi = [small[:, k, :, 3 * T:3 * T + 1] for k in range(XSLOTS)]
        maxo = [small[:, k, :, 3 * T + 1:3 * T + 2] for k in range(XSLOTS)]
        nmax = [small[:, k, :, 3 * T + 2:3 * T + 3] for k in range(XSLOTS)]
        part = [small[:, k, :, 3 * T + 3:3 * T + 4] for k in range(XSLOTS)]
        parto = [small[:, k, :, 3 * T + 4:3 * T + 5] for k in range(XSLOTS)]
        total = [small[:, k, :, 3 * T + 5:3 * T + 6] for k in range(XSLOTS)]
        recip = [small[:, k, :, 3 * T + 6:3 * T + 7] for k in range(XSLOTS)]

        bank = [ctx.enter_context(nc.psum_tensor(f"bank{k}", [P, 512], F32)) for k in range(8)]
        acc = bank[0:NB]
        turned = bank[3:3 + TB]
        side = bank[6:8]
        absolutes = bank[2:6]

        small_in = sem("small_in")
        w_in = sem("w_in")
        consts = sem("consts")
        vconsts = sem("vconsts")
        set_mm = sem("set_mm")
        set_ev = sem("set_ev")
        g_stored = sem("g_stored")
        g_in = sem("g_in")
        x_in = [sem(f"x_in{k}") for k in range(XSLOTS)]
        half_used = sem("half_used")
        dots_done = sem("dots_done")
        abs_done = sem("abs_done")
        exp_done = sem("exp_done")
        max_done = sem("max_done")
        prob_raw = sem("prob_raw")
        prob_done = sem("prob_done")
        weights_done = sem("weights_done")
        pool_out = sem("pool_out")
        fold_mm = sem("fold_mm")
        fold_ev = sem("fold_ev")
        chain_mm = sem("chain_mm")
        chain_ev = sem("chain_ev")
        link = sem("link")
        c_ready = sem("c_ready")
        c_used = sem("c_used")
        w7_in = [sem(f"w7_in{k}") for k in range(2)]
        w7_used = sem("w7_used")
        turned_done = sem("turned_done")
        cT_done = sem("cT_done")
        cL_done = sem("cL_done")
        wH_done = sem("wH_done")
        wL_done = sem("wL_done")
        split_used = sem("split_used")
        acc_done = sem("acc_done")
        f7_out = sem("f7_out")
        end_mm = sem("end_mm")
        end_ev = sem("end_ev")
        l_in = [sem(f"l_in{k}") for k in range(LSLOTS)]
        l_used = sem("l_used")
        out_stored = sem("out_stored")

        STEPS = (1, 2)
        CH_BT = sum(STEPS)
        SMALL_LOADS = 3 * 2 + 2 + 2
        W_LOADS = 5 * 2 + 3 + 2 * NCH
        FOLD = 6 * NCH + 1

        def at_tile(t, m):
            return t[:, m, :] if isinstance(m, int) else t[:, bass.ds(m, 1), :].rearrange("p o e -> p (o e)")

        x_v = x.rearrange("(s b) (f t) e -> s (b f) (t e)", b=UB, f=2)
        label_v = label.rearrange("(m p) (c r) e -> m p c (r e)", p=P, r=LR)
        out_v = out.rearrange("(m p) k -> m p k", p=P)
        row = lambda a: a.rearrange("(o e) -> o e", o=1)
        col = lambda a: a.rearrange("(e o) -> e o", o=1)

        class Tile:
            def __init__(self, i, k):
                self.i, self.k = i, k
                self.n = i * XBODY + k
                self.slot, self.half = k % XSLOTS, k % 2
                self.m = i * (XBODY // 2) + k // 2
                self.landed = (i * (XBODY // XSLOTS) + (k // XSLOTS + 1)) * 16
                self.first = isinstance(i, int) and k == 0
                self.second = isinstance(i, int) and k == 1

            def prev(self, d):
                return Tile(self.i, self.k - d)

        def chain_under(tile):
            if tile.half:
                return [(tile.m, 0, 0)]
            return [] if tile.first else [(tile.prev(1).m, 1, step) for step in range(STEPS[1])]

        def pooling_tiles(eng):
            for k in range(XPRE):
                yield Tile(0, k)
            with eng.Fori(0, XLOOPS) as i:
                for k in range(XPRE, XPRE + XBODY):
                    yield Tile(i, k)
            for k in range(NS - XPOST, NS):
                yield Tile(0, k)

        def split_chunk(g, k):
            return k // WC if k // WC < SPLIT[g] else None

        chunks0 = [NBLK * sum(SPLIT[:g]) for g in range(len(GROUPS))]

        block = ctx.enter_context(nc.Block())

        @block.sync
        def _(sp):
            def rows_in(dst, src, s):
                full = E // P
                sp.dma_start(dst[:, 0:full, :], src[0:full * P, :].rearrange("(c p) n -> p c n", p=P)).then_inc(s, 16)
                sp.dma_start(dst[0:E - full * P, full, :], src[full * P:E, :]).then_inc(s, 16)

            rows_in(w1nat[:, 0], w1, small_in)
            rows_in(w1nat[:, 1], w3, small_in)
            rows_in(vnat, v, small_in)
            sp.dma_start(w2sb[:, 0:1], w2).then_inc(small_in, 16)
            sp.dma_start(w2sb[:, 1:2], w4).then_inc(small_in, 16)
            sp.dma_start(w1T[:, 0, E:E + 1], col(b1)).then_inc(small_in, 16)
            sp.dma_start(w1T[:, 1, E:E + 1], col(b3)).then_inc(small_in, 16)
            sp.dma_start(xslot[0], x_v[0]).then_inc(x_in[0], 16)
            rows_in(w6nat, w6, w_in)
            rows_in(w8a, w8[0:E, :], w_in)
            rows_in(w5sb[:, 0:NCH], w5[0:E, :], w_in)
            rows_in(w5sb[:, NCH:2 * NCH], w5[E:2 * E, :], w_in)
            rows_in(w8b, w8[E:2 * E, :], w_in)
            for k, b in ((B5, b5), (B8, b8), (B7, b7)):
                sp.dma_start(brow[32 * k:32 * k + 1, :], row(b)).then_inc(w_in, 16)
            for k, b in enumerate((b5, b6)):
                for c, (o, n) in enumerate(CHUNKS):
                    sp.dma_start(bcol[0:n, k, c:c + 1], col(b)[o:o + n, :],
                                 allow_slow_non_contiguous=True).then_inc(w_in, 16)
            for n in range(1, XSLOTS):
                sp.dma_start(xslot[n], x_v[n]).then_inc(x_in[n], 16)

            sp.wait_ge(set_ev, 5 + NCH)
            share = -(-(E - 1) // (NS - XSLOTS))
            for n in range(XSLOTS, NS):
                sp.wait_ge(half_used, 2 * (n - XSLOTS + 1))
                sp.dma_start(xslot[n % XSLOTS], x_v[n]).then_inc(x_in[n % XSLOTS], 16)
                for i in range((n - XSLOTS) * share, min((n - XSLOTS + 1) * share, E - 1)):
                    sp.dma_start(gflat[:, row_start[i]:row_start[i + 1]],
                                 gram[i % P:i % P + 1, i // P, i + 1:E]).then_inc(g_stored, 16)

            sp.wait_ge(g_stored, 16 * (E - 1))
            sp.wait_ge(consts, 1)
            full = (NBLK - 1) * BLK
            sp.dma_start(gcol[:, 0:NBLK - 1, :],
                         gflat[:, 0:full].rearrange("o (n p k) -> p (o n) k", p=P, k=KB)).then_inc(g_in, 16)
            sp.dma_start(gcol[0:LASTP, NBLK - 1, :],
                         gflat[:, full:PAIRS].rearrange("o (p k) -> (o p) k", k=KB)).then_inc(g_in, 16)

            sp.wait_ge(half_used, 2 * NS)
            for c in range(LSLOTS):
                sp.wait_ge(w7_in[1], 16 * (c + 2))
                sp.dma_start(lslot[c], label_v[0, :, c]).then_inc(l_in[c], 16)
            for c in range(LSLOTS, LC):
                sp.wait_ge(l_used, c - LSLOTS + 1)
                sp.dma_start(lslot[c % LSLOTS], label_v[0, :, c]).then_inc(l_in[c % LSLOTS], 16)
            with sp.Fori(1, NBT) as m:
                for c in range(LC):
                    sp.wait_ge(l_used, m * LC + (c - LSLOTS + 1))
                    sp.dma_start(lslot[c % LSLOTS], label_v[bass.ds(m, 1), :, c].rearrange("o p c -> (o p) c")
                                 ).then_inc(l_in[c % LSLOTS], 16)

        @block.gpsimd
        def _(pool):
            ki = [0]

            def step(ins):
                ki[0] += 1
                ins.then_inc(consts, 1)
                pool.wait_ge(consts, ki[0])

            step(nc.gpsimd.memset(gcol[:], 0.0))
            step(nc.gpsimd.memset(ident[:], 0.0))
            step(nc.gpsimd.memset(onehot, 0.0))
            step(nc.gpsimd.affine_select(out=ident[:], in_=ident[:], compare_op=ALU.not_equal, fill=1.0,
                                         base=0, pattern=[[-1, P]], channel_multiplier=1))
            for f in range(2):
                step(nc.gpsimd.affine_select(out=onehot, in_=onehot, compare_op=ALU.not_equal,
                                             fill=1.0, base=-f, pattern=[[-2, UB]], channel_multiplier=1))

            for tile in pooling_tiles(pool):
                pool.wait_ge(prob_done, tile.n + 1)
                for h, (t0, t1) in enumerate(HALVES):
                    if not tile.first:
                        pool.wait_ge(half_used, tile.n * 2 + (h - 1))
                    nc.gpsimd.tensor_tensor(
                        weights[h],
                        prob[tile.slot][:, :, t0:t1].rearrange("p h t -> p t h").unsqueeze(3).to_broadcast(
                            [P, t1 - t0, 2, UB]),
                        onehot.unsqueeze(1).unsqueeze(1).to_broadcast([P, t1 - t0, 2, UB]),
                        ALU.mult).then_inc(weights_done, 1)

            for m in range(NBT):
                j = next(m - b0 for b0, nb in GROUPS if m < b0 + nb)
                pool.wait_ge(l_used, (m + 1) * LC)
                pool.dma_start(out_v[m], score[:, j, :]).then_inc(out_stored, 16)
            pool.wait_ge(out_stored, 16 * NBT)

        @block.tensor
        def _(pe):
            pe.wait_ge(consts, 6)
            pe.wait_ge(small_in, 16 * SMALL_LOADS)
            for hd in range(2):
                for c, (o, n) in enumerate(CHUNKS):
                    mm = pe.transpose(bank[2 + hd][0:HID, o:o + n], w1nat[0:n, hd, c, :], ident[0:n, 0:n])
                mm.then_inc(set_mm, 1)
            for c, (o, n) in enumerate(CHUNKS):
                mm = pe.transpose(bank[4][0:VC, o:o + n], vnat[0:n, c, :], ident[0:n, 0:n])
            mm.then_inc(set_mm, 1)
            pe.wait_ge(set_ev, 3)
            pe.wait_ge(vconsts, 3)
            for hd in range(2):
                pe.matmul(bank[6 + hd][:, 0:E + 1], w2bc[:, hd, :], w1T[:, hd, :],
                          start=True, stop=True).then_inc(set_mm, 1)
            for c, (o, n) in enumerate(CHUNKS):
                pe.matmul(bank[2 + c][0:n, 0:E], vT[:, o:o + n], vT, start=True, stop=True).then_inc(set_mm, 1)

            def tturn(dst, src):
                for c, (o, n) in enumerate(CHUNKS):
                    mm = pe.transpose(dst[0:n, c * P:(c + 1) * P], src[:, o:o + n], ident[:])
                return mm

            def spread_row(dst, k):
                o = 32 * k
                return pe.matmul(dst[:, 0:E], ones[o:o + 1, :], brow[o:o + 1, :], start=True, stop=False)

            def rows_mm(dst, lhs, rhs, bias, nlhs):
                mm = spread_row(dst, bias)
                for q in range(nlhs):
                    n = CHUNKS[q % NCH][1]
                    mm = pe.matmul(dst[:, 0:E], lhs(q)[0:n, :], rhs[0:n, q, :], start=False, stop=(q == nlhs - 1))
                return mm

            def chain(m, s, step):
                if step == 0:
                    pe.wait_ge(pool_out, m * 2 + s + 1)
                pe.wait_ge(chain_ev, m * CH_BT + s + step)
                dst = side[step % 2]
                if step == 0:
                    mm = tturn(dst, flat[:, s, :])
                else:
                    pools = lambda q: turnT[:, q % NCH, q // NCH, :]
                    rows_mm(dst, pools, w5sb, B5, 2 * NCH)
                    mm = rows_mm(side[0], pools, w568, B_OUT, 2 * NCH)
                mm.then_inc(chain_mm, 1)

            pe.wait_ge(w_in, 16 * W_LOADS)
            pe.wait_ge(set_ev, 5 + NCH)

            fold = bank[0:2] + bank[6:8]
            steps = iter(range(FOLD))

            def fold_step(made):
                j = next(steps)
                if max(made, j - len(fold) + 1) > 0:
                    pe.wait_ge(fold_ev, max(made, j - len(fold) + 1))
                return fold[j % len(fold)]

            for c, (o, n) in enumerate(CHUNKS):
                dst = fold_step(0)
                for q, (oq, nq) in enumerate(CHUNKS):
                    mm = pe.transpose(dst[0:n, oq:oq + nq], w6nat[0:nq, q, o:o + n], ident[0:nq, 0:nq])
                mm.then_inc(fold_mm, 1)
            for q, (oq, nq) in enumerate(CHUNKS):
                dst = fold_step(NCH)
                for c, (o, n) in enumerate(CHUNKS):
                    mm = pe.matmul(dst[0:nq, 0:E], w6T[0:n, c, oq:oq + nq], w8a[0:n, c, :],
                                   start=(c == 0), stop=(c == NCH - 1))
                mm.then_inc(fold_mm, 1)
            for hd in range(2):
                for c, (o, n) in enumerate(CHUNKS):
                    dst = fold_step(0)
                    for q, (oq, nq) in enumerate(CHUNKS):
                        mm = pe.transpose(dst[0:n, oq:oq + nq], w5sb[0:nq, hd * NCH + q, o:o + n],
                                          ident[0:nq, 0:nq])
                    mm.then_inc(fold_mm, 1)
            for hd in range(2):
                for q, (oq, nq) in enumerate(CHUNKS):
                    dst = fold_step(4 * NCH)
                    for c, (o, n) in enumerate(CHUNKS):
                        mm = pe.matmul(dst[0:nq, 0:E], w5T[0:n, hd, c, oq:oq + nq], w68[0:n, c, :],
                                       start=(c == 0), stop=(c == NCH - 1))
                    mm.then_inc(fold_mm, 1)
            dst = fold_step(2 * NCH)
            pe.matmul(dst[0:1, 0:E], ones[32 * B8:32 * B8 + 1, 0:1], brow[32 * B8:32 * B8 + 1, :],
                      start=True, stop=False)
            for k, w in ((0, w68), (1, w8a)):
                for c, (o, n) in enumerate(CHUNKS):
                    mm = pe.matmul(dst[0:1, 0:E], bcol[0:n, k, c:c + 1], w[0:n, c, :], start=False,
                                   stop=(k == 1 and c == NCH - 1))
            mm.then_inc(fold_mm, 1)
            pe.wait_ge(fold_ev, FOLD)
            for tile in pooling_tiles(pe):
                steps = chain_under(tile)
                if not tile.first and not tile.second:
                    pe.wait_ge(pool_out, tile.n - 1)
                for h, (t0, t1) in enumerate(HALVES):
                    pe.wait_ge(weights_done, tile.n * 2 + (h + 1))
                    for t in range(t0, t1):
                        mm = pe.matmul(bank[tile.half][:, 0:E], weights[h][:, t - t0],
                                       xslot[tile.slot][:, t, :], start=(t == 0), stop=(t == T - 1))
                        if t in PE_STEPS and steps:
                            chain(*steps.pop(0))
                    mm.then_inc(half_used, 1)
                assert not steps
            for step in range(STEPS[1]):
                chain(NBT - 1, 1, step)

            loads = [0, 0]
            for g, (b0, nb) in enumerate(GROUPS):
                blk0, tile0 = g * NBLK, g * NBLK * KB

                def turn(blk, k):
                    if k == 0:
                        pe.wait_ge(c_ready, blk[0] + (blk0 + blk[1] + 1))
                    q = (tile0 + blk[1] * KB + k) % TB
                    for b in range(nb):
                        mm = pe.transpose(turned[q][:, b * P:(b + 1) * P],
                                          cblk[(blk0 + blk[1]) % 2][:, b, k:BLK:KB], ident[:])
                    mm.then_inc(turned_done, 1)

                def contract(blk, i, k, landed, np_):
                    slot, q = (blk0 + blk) % 2, (tile0 + blk * KB + k) % TB
                    last = blk == NBLK - 1 and k == KB - 1
                    chunk = split_chunk(g, k)
                    if k == 0:
                        pe.wait_ge(w7_in[slot], landed)
                    if chunk is not None and k % WC == 0:
                        pe.wait_ge(wL_done, i * (BODY * SPLIT[g]) + (chunks0[g] + blk * SPLIT[g] + chunk + 1))
                    pe.wait_ge(cT_done, i * (BODY * KB) + (tile0 + blk * KB + k + 1))
                    if chunk is None:
                        passes = [(cT[q], w7blk[slot][:, k * E:(k + 1) * E])]
                    else:
                        wb, r = wHL[(chunks0[g] + blk * SPLIT[g] + chunk) % 2], k % WC
                        wh, wl = wb[:, 0, r * E:(r + 1) * E], wb[:, 1, r * E:(r + 1) * E]
                        passes = [(cHL[q][:, 0], wh), (cHL[q][:, 0], wl), (cHL[q][:, 1], wh)]
                    for j, (lhs, rhs) in enumerate(passes):
                        if j == 2:
                            pe.wait_ge(cL_done, i * (BODY * WC * SPLIT[g])
                                       + (WC * (chunks0[g] + blk * SPLIT[g]) + k + 1))
                        for b in range(nb):
                            mm = pe.matmul(acc[b][:, 0:E], lhs[0:np_, b * P:(b + 1) * P], rhs[0:np_, :],
                                           start=False, stop=last and j == len(passes) - 1)
                            if k == KB - 3 and j == 0 and b == 0:
                                mm.then_inc(c_used, 1)
                    if last:
                        mm.then_inc(acc_done, 1)
                    elif k == KB - 1:
                        mm.then_inc(w7_used, 1)
                    elif chunk is not None and k % WC == WC - 1:
                        mm.then_inc(split_used, 1)

                if g == 0:
                    pe.wait_ge(chain_ev, CH_BT * NBT)
                else:
                    pe.wait_ge(f7_out, b0)
                for b in range(nb):
                    mm = spread_row(acc[b], B7)
                    if g == 0 and b == 0:
                        mm.then_inc(split_used, 1)
                    if g == 0 and b == 1:
                        mm.then_inc(w7_used, 1)
                turn((0, 0), 0)
                turn((0, 0), 1)
                s0, s1 = blk0 % 2, (blk0 + 1) % 2

                def tile_step(i, blk, k, landed, np_):
                    ahead = blk * KB + k + 2
                    if not isinstance(i, int) or ahead < NBLK * KB:
                        turn((i * BODY, ahead // KB), ahead % KB)
                    contract(blk, i, k, landed, np_)

                with pe.Fori(0, LOOPS) as i:
                    for blk in range(BODY):
                        for k in range(KB):
                            tile_step(i, blk, k, (i * (BODY // 2) + (loads[(s0, s1)[blk % 2]] + blk // 2 + 1)) * 16, P)
                for blk in range(NBLK - REST, NBLK):
                    slot = (s0, s1)[blk % 2]
                    for k in range(KB):
                        if blk < NBLK - 1:
                            tile_step(0, blk, k, 16 * (loads[slot] + blk // 2 + 1), P)
                        else:
                            tile_step(0, blk, k, 16 * (loads[slot] + blk // 2 + 2), LASTP)
                loads[s0] += NBLK // 2 + 2
                loads[s1] += NBLK // 2

                for b in range(nb):
                    e = 2 * (b0 + b)
                    pe.wait_ge(f7_out, b0 + b + 1)
                    if e:
                        pe.wait_ge(end_ev, e)
                    tturn(side[0], flat[:, b, :]).then_inc(end_mm, 1)
                    pe.wait_ge(end_ev, e + 1)
                    pe.matmul(side[1][:, 0:E], ident[:], out8[:, b0 + b, :], start=True, stop=False)
                    for c, (_, n) in enumerate(CHUNKS):
                        mm = pe.matmul(side[1][:, 0:E], turn1[0:n, c, :], w8b[0:n, c, :],
                                       start=False, stop=(c == NCH - 1))
                    mm.then_inc(end_mm, 1)

        @block.scalar
        def _(act):
            def cp(dst, src):
                return nc.scalar.activation(dst, src, ACT.Copy)

            def absolute(tile, t):
                grp, r = t // AG, t % AG
                if r == 0 and not (tile.first and grp < 2):
                    act.wait_ge(abs_done, tile.n * AGS + (grp - 1))
                ins = nc.scalar.activation(absolutes[(tile.half + grp) % 2 * AG + r][:, 0:E],
                                           xslot[tile.slot][:, t, :], ACT.Abs,
                                           accum_out=absum[:, tile.slot, t:t + 1])
                if r == AG - 1 or t == T - 1:
                    ins.then_inc(abs_done, 1)

            def exps(tile):
                act.wait_ge(dots_done, (tile.n + 1) * (2 * DGS))
                for hd in range(2):
                    ins = nc.scalar.activation(expo[tile.slot][:, hd, :], dots[tile.slot][:, hd, :], ACT.Exp,
                                               bias=ubc[:, hd, E:E + 1])
                ins.then_inc(exp_done, 1)

            def softexp(tile):
                k = tile.slot
                act.wait_ge(max_done, tile.n + 1)
                for hd in range(2):
                    ins = nc.scalar.activation(prob[k][:, hd, :], expo[k][:, hd, :], ACT.Exp,
                                               bias=nmax[k][:, hd, :], accum_out=part[k][:, hd, :])
                ins.then_inc(prob_raw, 1)

            def turned_out(dst3, src):
                cp(dst3[:, 0:NCH - 1], src[:, 0:(NCH - 1) * P].rearrange("p (c b) -> p c b", b=P))
                n = CHUNKS[-1][1]
                return cp(dst3[0:n, NCH - 1], src[0:n, (NCH - 1) * P:NCH * P])

            def pools_turned(src, s):
                for c, (_, n) in enumerate(CHUNKS):
                    ins = cp(turnT[0:n, c, :, s * UB:(s + 1) * UB],
                             src[0:n, c * P:(c + 1) * P].rearrange("p (h b) -> p h b", h=2))
                return ins

            def chain_out(m, s, step):
                act.wait_ge(chain_mm, m * CH_BT + (s + step + 1))
                src = side[step % 2]
                if step == 0:
                    ins = pools_turned(src, s)
                else:
                    cp(at_tile(h_all, m), src[:, 0:E])
                    ins = cp(at_tile(out8, m), side[0][:, 0:E])
                ins.then_inc(chain_ev, 1)

            def pools_out(m, s):
                act.wait_ge(half_used, m * 4 + (2 * s + 2))
                cp(flat[:, s, :], bank[s][:, 0:E]).then_inc(pool_out, 1)

            def fold_outs():
                fold = bank[0:2] + bank[6:8]
                places = [w6T[0:n, c, :] for c, (_, n) in enumerate(CHUNKS)]
                places += [w68[0:n, c, :] for c, (_, n) in enumerate(CHUNKS)]
                places += [w5T[0:n, hd, c, :] for hd in range(2) for c, (_, n) in enumerate(CHUNKS)]
                places += [w568[0:n, hd * NCH + c, :] for hd in range(2) for c, (_, n) in enumerate(CHUNKS)]
                places += [brow[32 * B_OUT:32 * B_OUT + 1, :]]
                for j, place in enumerate(places):
                    act.wait_ge(fold_mm, j + 1)
                    cp(place, fold[j % len(fold)][0:place.shape[0], 0:E]).then_inc(fold_ev, 1)
                    yield

            full = (NBLK - 1) * BLK
            w7_v = w7[0:full, :].rearrange("(n p k) e -> n p (k e)", p=P, k=KB)
            w7_last = w7[full:PAIRS, :].rearrange("(p k) e -> p (k e)", k=KB)

            def load(slot, blk):
                act.dma_start(w7blk[slot], w7_v[blk] if isinstance(blk, int) else
                              w7_v[bass.ds(blk, 1)].rearrange("o p c -> (o p) c")).then_inc(w7_in[slot], 16)

            def load_last(slot):
                cut = LASTP // 16 * 16
                act.dma_start(w7blk[slot][0:cut], w7_last[0:cut]).then_inc(w7_in[slot], 16)
                act.dma_start(w7blk[slot][cut:LASTP], w7_last[cut:LASTP]).then_inc(w7_in[slot], 16)

            act.wait_ge(set_ev, 5 + NCH)
            fold_out = fold_outs()
            for tile in pooling_tiles(act):
                before = [] if tile.first else [tile.prev(1)]
                chains = chain_under(before[0]) if before else []
                late = chain_under(tile.prev(2))[1:] if before and not before[0].first else []
                if before:
                    exps(before[0])
                act.wait_ge(x_in[tile.slot], tile.landed)
                for t in range(T):
                    absolute(tile, t)
                    if tile.first and t >= FOLD_AT or tile.second and EXP_AT < t <= EXP_AT + FOLD - (T - FOLD_AT):
                        next(fold_out)
                    if t == EXP_AT and before:
                        softexp(before[0])
                    if t == LATE_AT and late:
                        chain_out(*late[0])
                    if t == OUT_AT and before and not before[0].first:
                        pools_out(tile.prev(2).m, tile.half)
                    if t == TURN_AT and chains:
                        chain_out(*chains[0])
            exps(Tile(0, NS - 1))
            softexp(Tile(0, NS - 1))
            chain_out(NBT - 2, 1, 1)
            pools_out(NBT - 1, 0)
            load(0, 0)
            for step in chain_under(Tile(0, NS - 1)):
                chain_out(*step)
            pools_out(NBT - 1, 1)
            for step in range(STEPS[1]):
                chain_out(NBT - 1, 1, step)

            act.wait_ge(g_in, 32)
            loads = [0, 0]
            for g, (b0, nb) in enumerate(GROUPS):
                blk0, tile0, used = g * NBLK, g * NBLK * KB, g * (NBLK - 1)
                s0, s1 = blk0 % 2, (blk0 + 1) % 2

                def scaled(tiles, blk, k, gblk, np_):
                    act.wait_ge(turned_done, tiles + (tile0 + blk * KB + k + 1))
                    q = (tile0 + blk * KB + k) % TB
                    dst = cT[q] if split_chunk(g, k) is None else cHL[q][:, 0]
                    nc.scalar.activation(dst[0:np_, 0:nb * P], turned[q][0:np_, 0:nb * P], ACT.Copy,
                                         scale=gblk[0:np_, k:k + 1]).then_inc(cT_done, 1)

                def w7_high(i, blk, chunk, landed, np_=P):
                    c = chunks0[g] + blk * SPLIT[g] + chunk
                    if chunk == 0:
                        act.wait_ge(w7_in[(blk0 + blk) % 2], landed)
                    if c > 0:
                        act.wait_ge(split_used, i * (BODY * SPLIT[g]) + c)
                    nc.scalar.activation(wHL[c % 2][0:np_, 0, :],
                                         w7blk[(blk0 + blk) % 2][0:np_, chunk * WC * E:(chunk + 1) * WC * E],
                                         ACT.Copy).then_inc(wH_done, 1)

                def w7_highs(i, blk, k, landed, np_=P, np_next=P):
                    if k % WC == 1 and k // WC + 1 < SPLIT[g]:
                        w7_high(i, blk, k // WC + 1, None, np_)
                    if k == KNEXT and landed is not None:
                        w7_high(i, blk + 1, 0, landed, np_next)

                l0, l1 = 16 * loads[s0], 16 * loads[s1]
                w7_high(0, 0, 0, l0 + 16)

                with act.Fori(0, LOOPS) as i:
                    for blk in range(BODY):
                        for k in range(KB):
                            scaled(i * (BODY * KB), blk, k, at_tile(gcol, i * BODY + blk), P)
                            nxt = blk + 1
                            w7_highs(i, blk, k, (i * (BODY // 2) + (nxt // 2 + 1)) * 16 + (l0, l1)[nxt % 2])
                            if k == 2:
                                act.wait_ge(w7_used, i * BODY + (used + blk + 1))
                                load((s0, s1)[nxt % 2], i * BODY + nxt)
                for blk in range(NBLK - REST, NBLK):
                    for k in range(KB):
                        scaled(0, blk, k, gcol[:, blk, :], P if blk < NBLK - 1 else LASTP)
                        nxt = blk + 1
                        landed = (l0, l1)[nxt % 2] + 16 * (nxt // 2 + (1 if nxt < NBLK - 1 else 2))
                        w7_highs(0, blk, k, landed if nxt < NBLK else None,
                                 P if blk < NBLK - 1 else LASTP, P if blk < NBLK - 2 else LASTP)
                        if k == 2:
                            act.wait_ge(w7_used, used + blk + 1)
                            if nxt < NBLK - 1:
                                load((s0, s1)[nxt % 2], nxt)
                            elif nxt == NBLK - 1:
                                load_last(s0)
                            elif g + 1 < len(GROUPS):
                                load(s1, 0)

                loads[s0] += NBLK // 2 + 2
                loads[s1] += NBLK // 2

                act.wait_ge(acc_done, g + 1)
                for b in range(nb):
                    cp(flat[:, b, :], acc[b][:, 0:E]).then_inc(f7_out, 1)
                for b in range(nb):
                    e = 2 * (b0 + b)
                    act.wait_ge(end_mm, e + 1)
                    turned_out(turn1, side[0]).then_inc(end_ev, 1)
                    act.wait_ge(end_mm, e + 2)
                    cp(out8[:, b0 + b, :], side[1][:, 0:E]).then_inc(end_ev, 1)

        @block.vector
        def _(dve):
            nc.vector.memset(ones[:], 1.0).then_inc(vconsts, 1)
            nc.vector.memset(padv[:], PAD).then_inc(vconsts, 1)
            dve.wait_ge(small_in, 16 * SMALL_LOADS)
            nc.vector.tensor_copy(w2bc, w2sb[:].unsqueeze(2).to_broadcast([HID, 2, P])).then_inc(vconsts, 1)
            for hd in range(2):
                dve.wait_ge(set_mm, hd + 1)
                nc.vector.tensor_copy(w1T[:, hd, 0:E], bank[2 + hd][0:HID, 0:E]).then_inc(set_ev, 1)
            dve.wait_ge(set_mm, 3)
            nc.vector.tensor_copy(vT, bank[4][0:VC, 0:E]).then_inc(set_ev, 1)
            for hd in range(2):
                dve.wait_ge(set_mm, 4 + hd)
                nc.vector.tensor_copy(ubc[:, hd, :], bank[6 + hd][:, 0:E + 1]).then_inc(set_ev, 1)
            for c, (o, n) in enumerate(CHUNKS):
                dve.wait_ge(set_mm, 6 + c)
                nc.vector.tensor_copy(gram[0:n, c, :], bank[2 + c][0:n, 0:E]).then_inc(set_ev, 1)
            dve.wait_ge(set_ev, 5 + NCH)

            SWAP = [q ^ 1 for q in range(32)]

            def score_row(tile, q):
                hd, t = q // T, q % T
                grp, r = hd * DGS + t // DG, t % DG
                if r == 0 and not (tile.first and grp < 2):
                    dve.wait_ge(dots_done, tile.n * (2 * DGS) + (grp - 1))
                ins = nc.vector.scalar_tensor_tensor(
                    out=products[:, grp % 2, r, :], in0=xslot[tile.slot][:, t, :], scalar=1.0,
                    in1=ubc[:, hd, 0:E], op0=ALU.mult, op1=ALU.mult,
                    accum_out=dots[tile.slot][:, hd, t:t + 1])
                if r == DG - 1 or t == T - 1:
                    ins.then_inc(dots_done, 1)

            LINKS = 8

            def linked(ins, n, j):
                ins.then_inc(link, 1)
                dve.wait_ge(link, n * LINKS + j)

            def carry():
                nc.vector.memset(tick[:], 0.0)

            def maxima(n, k):
                dve.wait_ge(exp_done, n + 1)
                dve.wait_ge(abs_done, (n + 1) * AGS)
                linked(nc.vector.tensor_scalar(masked[:, k, :], absum[:, k, :], 0.0, None, ALU.is_equal), n, 1)
                carry()
                for hd in range(2):
                    ins = nc.vector.copy_predicated(expo[k][:, hd, :], masked[:, k, :].bitcast(U32),
                                                    padv[:].to_broadcast([P, T]))
                linked(ins, n, 2)
                linked(nc.vector.tensor_reduce(maxi[k], expo[k], AX.X, ALU.max), n, 3)
                carry()
                linked(nc.vector.stream_shuffle(maxo[k], maxi[k], SWAP), n, 4)
                linked(nc.vector.tensor_tensor(maxi[k], maxi[k], maxo[k], ALU.max), n, 5)
                nc.vector.tensor_scalar(nmax[k], maxi[k], -1.0, None, ALU.mult).then_inc(max_done, 1)

            def normalise(n, k):
                dve.wait_ge(prob_raw, n + 1)
                carry()
                linked(nc.vector.stream_shuffle(parto[k], part[k], SWAP), n, 6)
                linked(nc.vector.tensor_tensor(total[k], part[k], parto[k], ALU.add), n, 7)
                linked(nc.vector.reciprocal(recip[k], total[k]), n, 8)
                nc.vector.tensor_tensor(prob[k], prob[k], recip[k].to_broadcast([P, 2, T]),
                                        ALU.mult).then_inc(prob_done, 1)

            for tile in pooling_tiles(dve):
                dve.wait_ge(x_in[tile.slot], tile.landed)
                for q in range(2 * T):
                    score_row(tile, q)
                    if not tile.first and q == MAX_AT:
                        maxima(tile.prev(1).n, tile.prev(1).slot)
                    if not tile.first and q == NORM_AT:
                        normalise(tile.prev(1).n, tile.prev(1).slot)
            maxima(NS - 1, (NS - 1) % XSLOTS)
            normalise(NS - 1, (NS - 1) % XSLOTS)

            def label_row(m, j, q):
                c, r = q // LR, q % LR
                row_in = lslot[c % LSLOTS][:, r, :]
                if r == 0:
                    dve.wait_ge(l_in[c % LSLOTS], m * (16 * LC // LSLOTS) + 16 * (c // LSLOTS + 1))
                ins = nc.vector.scalar_tensor_tensor(
                    out=row_in, in0=row_in, scalar=1.0, in1=out8[:, m, :], op0=ALU.mult, op1=ALU.mult,
                    accum_out=score[:, j, q:q + 1])
                if r == LR - 1:
                    ins.then_inc(l_used, 1)

            def rows_of(blk):
                lo, hi = blk * BLK, min((blk + 1) * BLK, PAIRS)
                return [(i, max(lo, row_start[i]), min(hi, row_start[i + 1])) for i in range(E - 1)
                        if max(lo, row_start[i]) < min(hi, row_start[i + 1])]

            def pair_row(g, blk, r):
                b0, nb = GROUPS[g]
                gblk, rows = g * NBLK + blk, rows_of(blk)
                i, a, z = rows[r]
                j, n = i + 1 + a - row_start[i], z - a
                if r == 0 and gblk >= 2:
                    dve.wait_ge(c_used, gblk - 1)
                dst = cblk[gblk % 2][:, 0:nb, a - blk * BLK:z - blk * BLK]
                if nb * (60 + n / 2) < 60 + nb * n:
                    for b in range(nb):
                        ins = nc.vector.tensor_scalar(dst[:, b], h_all[:, b0 + b, j:j + n],
                                                      h_all[:, b0 + b, i:i + 1], None, ALU.mult)
                else:
                    ins = nc.vector.tensor_tensor(dst, h_all[:, b0:b0 + nb, j:j + n],
                                                  h_all[:, b0:b0 + nb, i:i + 1].to_broadcast([P, nb, n]),
                                                  ALU.mult)
                if r == len(rows) - 1:
                    ins.then_inc(c_ready, 1)

            def w7_low(g, blk, chunk, np_):
                c = chunks0[g] + blk * SPLIT[g] + chunk
                dve.wait_ge(wH_done, c + 1)
                wb = wHL[c % 2]
                nc.vector.tensor_tensor(wb[0:np_, 1, :],
                                        w7blk[(g * NBLK + blk) % 2][0:np_, chunk * WC * E:(chunk + 1) * WC * E],
                                        wb[0:np_, 0, :].bitcast(F32), ALU.subtract).then_inc(wL_done, 1)

            def cross_low(g, blk, k, np_):
                nb = GROUPS[g][1]
                t = g * NBLK * KB + blk * KB + k
                dve.wait_ge(cT_done, t + 1)
                nc.vector.scalar_tensor_tensor(
                    out=cHL[t % TB][0:np_, 1, 0:nb * P], in0=turned[t % TB][0:np_, 0:nb * P],
                    scalar=gcol[0:np_, blk, k:k + 1], in1=cHL[t % TB][0:np_, 0, 0:nb * P].bitcast(F32),
                    op0=ALU.mult, op1=ALU.subtract).then_inc(cL_done, 1)

            dve.wait_ge(g_stored, 16 * (E - 1))
            dve.wait_ge(half_used, 2 * NS - 1)
            for r in range(len(rows_of(0))):
                pair_row(0, 0, r)
            dve.wait_ge(chain_ev, CH_BT * NBT)
            dve.wait_ge(g_in, 32)
            def load_of(g, blk):
                nb = GROUPS[g][1]
                pairs = sum(min(nb * (60 + (z - a) / 2), 60 + nb * (z - a))
                            for _, a, z in rows_of((blk + 1) % NBLK))
                if g + 1 == len(GROUPS) and blk + 1 == NBLK:
                    pairs = 0
                return SPLIT[g] * (60 + WC * E) + SPLIT[g] * WC * (120 + nb * P) + pairs

            def label_plan(g):
                labels, row = GROUPS[g - 1][1] * K, 66 + E
                loads = [load_of(g, blk) for blk in range(NBLK)]
                share = [(KB - OUT8_BY) / KB] + [1] * (NBLK - 1)
                level = max(loads)
                room = lambda: [max(0, level - x) * f for x, f in zip(loads, share)]
                while sum(room()) > labels * row:
                    level -= 1
                while sum(room()) < labels * row:
                    level += 1
                plan, owed = [], 0.0
                for x in room():
                    owed += x / row
                    plan.append(min(int(owed + 0.5), labels - sum(plan)))
                    owed -= plan[-1]
                plan[-1] += labels - sum(plan)
                return plan

            for g in range(len(GROUPS)):
                p0, pn = GROUPS[g - 1] if g else (0, 0)
                plan = label_plan(g) if g else [0] * NBLK
                w7_low(g, 0, 0, P)
                for blk in range(NBLK):
                    np_ = P if blk < NBLK - 1 else LASTP
                    g1, blk1 = (g, blk + 1) if blk + 1 < NBLK else (g + 1, 0)
                    rows1 = len(rows_of(blk1)) if g1 < len(GROUPS) else 0
                    for k in range(KB):
                        if split_chunk(g, k) is not None:
                            cross_low(g, blk, k, np_)
                        if k % WC == 1 and k // WC + 1 < SPLIT[g]:
                            w7_low(g, blk, k // WC + 1, np_)
                        if k == KNEXT and blk + 1 < NBLK:
                            w7_low(g, blk + 1, 0, P if blk + 2 < NBLK else LASTP)
                        for r in range(rows1 * min(k, PAIRS_BY) // PAIRS_BY,
                                       rows1 * min(k + 1, PAIRS_BY) // PAIRS_BY):
                            pair_row(g1, blk1, r)
                        if g and blk == 0 and k == OUT8_BY:
                            dve.wait_ge(end_ev, 2 * (p0 + pn))
                            if p0:
                                dve.wait_ge(out_stored, 16 * p0)
                        done, k0 = sum(plan[:blk]), OUT8_BY if blk == 0 else 0
                        for q in range(done + plan[blk] * max(k - k0, 0) // (KB - k0),
                                       done + plan[blk] * max(k + 1 - k0, 0) // (KB - k0)):
                            label_row(p0 + q // K, q // K, q % K)

            p0, pn = GROUPS[-1]
            dve.wait_ge(end_ev, 2 * (p0 + pn))
            dve.wait_ge(out_stored, 16 * p0)
            for j in range(pn):
                for q in range(K):
                    label_row(p0 + j, j, q)


_ORDER = ["r_x", "r_label_embedding"] + ["L0_rec_" + n for n in
          ("w1", "b1", "w2", "w3", "b3", "w4", "w5", "b5", "w6", "b6", "w7", "b7", "w8", "b8", "v")]


def kernel(**inputs):
    import numpy as np
    import concourse.bacc as bacc
    from concourse.bass_utils import run_bass_kernel_spmd

    nc = bacc.Bacc("TRN2", target_bir_lowering=False, num_devices=1)
    arrays, args = {}, []
    for name in _ORDER:
        a = np.ascontiguousarray(inputs[name])
        arrays[f"in_{name}"] = a
        args.append(nc.dram_tensor(f"in_{name}", a.shape, mybir.dt.from_np(a.dtype), kind="ExternalInput").ap())
    users, labels = inputs["r_label_embedding"].shape[:2]
    args.append(nc.dram_tensor("scores", (users, labels), F32, kind="ExternalOutput").ap())
    rec_kernel(nc, *args)
    r = run_bass_kernel_spmd(nc, [arrays], core_ids=[0])
    return r.results[0]["scores"]
```
